# Optimizing a Trainium2 kernel written in Bass

```python
import numpy as np
import jax
import jax.numpy as jnp

def _softmax(x, axis=-1):
    return jax.nn.softmax(x, axis=axis)

def _gelu(x):
    return jax.nn.gelu(x, approximate=True)

def _silu(x):
    return jax.nn.silu(x)

def _sigmoid(x):
    return jax.nn.sigmoid(x)

def _layernorm(x, axis=-1, eps=1e-05):
    m = jnp.mean(x, axis=axis, keepdims=True)
    v = jnp.var(x, axis=axis, keepdims=True)
    return (x - m) / jnp.sqrt(v + eps)

def _scatter_add(tgt, idx, src, axis=0):
    return tgt.at[idx].add(src)

def _segment_sum(src, seg, n):
    return jax.ops.segment_sum(src, seg, n)
kernel_name = 'mk_seq_postln_d1_jaxref_r8_964969'

def setup_inputs(seed: int=0):
    np.random.seed(seed)
    _w = jnp.asarray

    def _L0_attn_setup():
        import jax, jax.numpy as jnp
        import numpy as np
        B, T, C = (64, 32, 128)
        N_HEAD, HEAD_SIZE, KV_RANK = (16, 64, 128)
        BLOCK_SIZE = 32
        key = jax.random.key(seed)
        ks = jax.random.split(key, 5)
        HD = N_HEAD * HEAD_SIZE

        def init(k, shape):
            fan_in = shape[0]
            bound = 1.0 / np.sqrt(fan_in)
            return jax.random.uniform(k, shape, jnp.float32, -bound, bound)
        return {'x': jax.random.normal(ks[0], (B, T, C), jnp.float32), 'w_kv_down': init(ks[1], (C, KV_RANK)), 'w_kv_up': init(ks[2], (KV_RANK, 2 * HD)), 'w_q': init(ks[3], (C, HD)), 'w_out': init(ks[4], (HD, C))}
    _L0_attn_in = _L0_attn_setup()

    def _L0_ffn_setup():
        import jax, jax.numpy as jnp
        import numpy as np
        BLOCK = 16
        _GRID = jnp.array([0.0, 0.5, 1.0, 1.5, 2.0, 3.0, 4.0, 6.0], dtype=jnp.float32)
        _MID = jnp.array([0.25, 0.75, 1.25, 1.75, 2.5, 3.5, 5.0], dtype=jnp.float32)

        def fp4_quant_dequant(x):
            shape = x.shape
            xb = x.reshape(shape[:-1] + (shape[-1] // BLOCK, BLOCK))
            scale = jnp.max(jnp.abs(xb), axis=-1, keepdims=True) / 6.0
            scale = jnp.maximum(scale, jnp.float32(1e-12))
            xn = xb / scale
            idx = jnp.searchsorted(_MID, jnp.abs(xn))
            q = _GRID[idx] * jnp.sign(xn) * scale
            return q.reshape(shape)

        def fp4_linear(x, w):
            xq = fp4_quant_dequant(x)
            wq = fp4_quant_dequant(w)
            return jnp.einsum('bsk,nk->bsn', xq, wq)
        key = jax.random.key(seed)
        k1, k2, k3, k4 = jax.random.split(key, 4)
        H, I = (128, 352)
        x = jax.random.normal(k1, (4, 512, H), dtype=jnp.float32)
        w_gate = jax.random.normal(k2, (I, H), dtype=jnp.float32) * 0.02
        w_up = jax.random.normal(k3, (I, H), dtype=jnp.float32) * 0.02
        w_down = jax.random.normal(k4, (H, I), dtype=jnp.float32) * 0.02
        return {'x': x, 'w_gate': w_gate, 'w_up': w_up, 'w_down': w_down}
    _L0_ffn_in = _L0_ffn_setup()
    _d = {'L0_attn_x': _L0_attn_in['x'], 'L0_attn_w_kv_down': _L0_attn_in['w_kv_down'], 'L0_attn_w_kv_up': _L0_attn_in['w_kv_up'], 'L0_attn_w_q': _L0_attn_in['w_q'], 'L0_attn_w_out': _L0_attn_in['w_out'], 'L0_ffn_w_gate': _L0_ffn_in['w_gate'], 'L0_ffn_w_up': _L0_ffn_in['w_up'], 'L0_ffn_w_down': _L0_ffn_in['w_down']}
    _x0 = _d['L0_attn_x']
    _d['L0_attn_x'] = jax.random.normal(jax.random.fold_in(jax.random.key(seed), 1), (1, 2048, 128), dtype=_x0.dtype)
    del _x0
    return _d

def reference(L0_attn_x, L0_attn_w_kv_down, L0_attn_w_kv_up, L0_attn_w_q, L0_attn_w_out, L0_ffn_w_gate, L0_ffn_w_up, L0_ffn_w_down):

    def _L0_attn_ref(x, w_kv_down, w_kv_up, w_q, w_out):
        import jax, jax.numpy as jnp
        import numpy as np
        B, T, C = (64, 32, 128)
        N_HEAD, HEAD_SIZE, KV_RANK = (16, 64, 128)
        BLOCK_SIZE = 32
        Bx, Tx, Cx = x.shape
        HD = N_HEAD * HEAD_SIZE
        latent_kv = x @ w_kv_down
        kv = latent_kv @ w_kv_up
        k, v = (kv[..., :HD], kv[..., HD:])
        k = k.reshape(Bx, Tx, N_HEAD, HEAD_SIZE)
        v = v.reshape(Bx, Tx, N_HEAD, HEAD_SIZE)
        q = (x @ w_q).reshape(Bx, Tx, N_HEAD, HEAD_SIZE)
        scale = HEAD_SIZE ** (-0.5)
        att = jnp.einsum('bqhd,bkhd->bhqk', q, k) * scale
        causal = jnp.tril(jnp.ones((Tx, Tx), dtype=bool))
        att = jnp.where(causal, att, -jnp.inf)
        att = jax.nn.softmax(att, axis=-1)
        y = jnp.einsum('bhqk,bkhd->bqhd', att, v)
        y = y.reshape(Bx, Tx, HD)
        return y @ w_out

    def _L0_ffn_ref(x, w_gate, w_up, w_down):
        import jax, jax.numpy as jnp
        import numpy as np
        BLOCK = 16
        _GRID = jnp.array([0.0, 0.5, 1.0, 1.5, 2.0, 3.0, 4.0, 6.0], dtype=jnp.float32)
        _MID = jnp.array([0.25, 0.75, 1.25, 1.75, 2.5, 3.5, 5.0], dtype=jnp.float32)

        def fp4_quant_dequant(x):
            shape = x.shape
            xb = x.reshape(shape[:-1] + (shape[-1] // BLOCK, BLOCK))
            scale = jnp.max(jnp.abs(xb), axis=-1, keepdims=True) / 6.0
            scale = jnp.maximum(scale, jnp.float32(1e-12))
            xn = xb / scale
            idx = jnp.searchsorted(_MID, jnp.abs(xn))
            q = _GRID[idx] * jnp.sign(xn) * scale
            return q.reshape(shape)

        def fp4_linear(x, w):
            xq = fp4_quant_dequant(x)
            wq = fp4_quant_dequant(w)
            return jnp.einsum('bsk,nk->bsn', xq, wq)
        gate = fp4_linear(x, w_gate)
        y = fp4_linear(x, w_up)
        h = jax.nn.silu(gate) * y
        return fp4_linear(h, w_down)
    x = L0_attn_x
    x = _layernorm(x + _L0_attn_ref(x, L0_attn_w_kv_down, L0_attn_w_kv_up, L0_attn_w_q, L0_attn_w_out), axis=-1)
    x = _layernorm(x + _L0_ffn_ref(x, L0_ffn_w_gate, L0_ffn_w_up, L0_ffn_w_down), axis=-1)
    return x

_drawn_inputs = setup_inputs


def setup_inputs(seed=0):
    import zlib

    import numpy as np

    out = dict(_drawn_inputs(seed))
    spreads = {}
    factors = {'L0_attn_w_kv_down': 4.28,
     'L0_attn_w_kv_up': 4.173,
     'L0_attn_w_q': 8.0,
     'L0_attn_w_out': 4.515,
     'L0_ffn_w_gate': 5.556,
     'L0_ffn_w_up': 5.286,
     'L0_ffn_w_down': 5.302}
    for name, (base, spread) in spreads.items():
        noise = np.random.default_rng([zlib.crc32(name.encode()), seed]).standard_normal(out[name].shape)
        drawn = base * np.exp(spread * noise) if base else spread * noise
        out[name] = jnp.asarray(drawn.astype(out[name].dtype))
    for name, factor in factors.items():
        out[name] = (out[name] * factor).astype(out[name].dtype)
    return out
```

```python
import concourse.bass as bass
from concourse import mybir
from contextlib import ExitStack

F32 = mybir.dt.float32
F32R = mybir.dt.float32r
BF16 = mybir.dt.bfloat16
U32 = mybir.dt.uint32
ALU = mybir.AluOpType
ACT = mybir.ActivationFunctionType
AX = mybir.AxisListType

P = 128
T = 2048
C = 128
NT = T // P
HEADS, HEAD = 16, 64
HD = HEADS * HEAD
PAIRS = HEADS // 2
SCALE = HEAD ** -0.5
GT = 2
NG = NT // GT
GQ = GT * P
CH = 1024
BANK = 512
FF = 352
BLK = 16
FFK = [(0, 128), (128, 128), (256, 96)]
EPS = 1e-5
MASKED = -3.0e38
FP4_MAX = 6.0
HALF_MAGIC = 1.5 * 2 ** 22
ONE_MAGIC = 1.5 * 2 ** 23
TWO_MAGIC = 1.5 * 2 ** 24
BELOW_ONE = 1.0 - 2.0 ** -23


def chunks(i):
    width = (i + 1) * P
    return [(a, min(CH, width - a)) for a in range(0, width, CH)]


LAG = 3


def pair_plan(last):
    plan = [("V", 0), ("V", 1)]
    turns, rest = [], []
    for g in range(NG):
        scores = []
        for i in range(GT * g, GT * (g + 1)):
            for h in range(2):
                for c in range(len(chunks(i))):
                    scores.append(("S", i, h, c))
                    if i == GT * g + 1 and h == 0 and c == 0:
                        scores.append(("N", i - 1))
        if g:
            scores.insert(1, ("N", GT * g - 1))
        done = 0
        n = len(scores)
        for k, s in enumerate(scores):
            plan.append(s)
            want = len(turns) * max(0, k + 1 - LAG) // max(1, n - LAG)
            while done < want:
                plan.append(turns[done])
                done += 1
        plan += turns[done:]
        turns = [("T", g, j) for j in range(GT * g + GT)] + [("Y", g), ("O", g)]
    tail = [] if last else [("P", "q", 0), ("P", "q", 1), ("P", "k", 0), ("P", "k", 1)]
    plan += tail[:1] + [("N", NT - 1)] + tail[1:2]
    tail = tail[2:]
    for k, t in enumerate(turns):
        plan.append(t)
        if k in (1, 3) and tail:
            plan.append(tail.pop(0))
    return plan


def ffn_plan():
    plan = [("FW",)]
    for k in range(NG + 2):
        plan += [("FA", k), ("FB", k)] if k < NG else []
        plan += [("FH", k - 1), ("FD", k - 1)] if 0 < k <= NG else []
        plan += [("FE", k - 2)] if k >= 2 else []
    return plan


def numbers(plan):
    slot, turn, chunk, scaled = {}, {}, {}, {}
    ns = nt = nc_ = nn = 0
    for it in plan:
        if it[0] in ("V", "S", "P"):
            slot[it] = ns
            ns += 1
        if it[0] == "S":
            chunk[it] = nc_
            nc_ += 1
        if it[0] == "T":
            turn[it[1:]] = nt
            nt += 1
        if it[0] == "N":
            for c in range(len(chunks(it[1]))):
                for h in range(2):
                    nn += 1
                    scaled[(it[1], h, c)] = nn
        if it[0] == "FB":
            for t in range(GT):
                slot[("F", it[1], t)] = ns
                ns += 1
            turn[("x", it[1])] = nt
            nt += 1
        if it[0] == "FD":
            for t in range(GT):
                turn[("h", it[1], t)] = nt
                nt += 1
        if it[0] == "FW":
            for w in range(3):
                turn[("w", w)] = nt
                nt += 1
    return slot, turn, chunk, scaled


def block_kernel(nc, x, w_kv_down, w_kv_up, w_q, w_out, w_gate, w_up, w_down, out):
    pair = pair_plan(False)
    final = pair_plan(True) + ffn_plan()
    SLOT, TURN, CHUNK, SCALED = numbers(pair)
    FSLOT, FTURN, FCHUNK, FSCALED = numbers(final)
    HEAD_SLOTS = 8
    SLOTS = 2 + sum(len(chunks(i)) * 2 for i in range(NT)) + 4
    TURNS = sum(GT * g + GT for g in range(NG))
    CHUNKS = SLOTS - 6
    assert SLOTS % 2 == 0 and TURNS % 6 == 0
    NORMS = CHUNKS
    TWO = [i for i in range(NT) if len(chunks(i)) == 2]
    LAST = PAIRS - 1

    x_t = x.rearrange("a (n p) c -> p (a n) c", p=P)
    out_t = out.rearrange("a (n p) c -> p (a n) c", p=P)

    with ExitStack() as ctx:
        def sb(name, shape, dt=F32):
            return ctx.enter_context(nc.sbuf_tensor(name, shape, dt))

        def psum(name, shape, dt=F32):
            return ctx.enter_context(nc.psum_tensor(name, shape, dt))

        def sem(name):
            return ctx.enter_context(nc.semaphore(name))

        resid = sb("resid", [P, NT, C])
        xT = sb("xT", [C, T])
        latT = sb("latT", [C, T])
        q_st = [sb(f"q_st{h}", [P, T], F32R) for h in range(2)]
        k_st = [sb(f"k_st{h}", [P, T], F32R) for h in range(2)]
        k_sw = [sb(f"k_sw{h}", [P, T], F32R) for h in range(2)]
        q_lo = sb("q_lo", [P, T], F32R)
        v = sb("v", [P, NT, P])
        probs = [sb(f"probs{k}", [P, GT, 2, T]) for k in range(2)]
        turned = [sb(f"turned{k}", [P, 2, GQ]) for k in range(3)]
        yT = [sb(f"yT{k}", [P, GQ]) for k in range(2)]
        ident = sb("ident", [P, P])
        ident_b = sb("ident_b", [P, P], BF16)
        mask = sb("mask", [P, P])
        mask_b = sb("mask_b", [P, P], BF16)
        w_d = sb("w_d", [C, C])
        w_qp = sb("w_qp", [C, P])
        w_kp = sb("w_kp", [C, P])
        w_vp = sb("w_vp", [C, P])
        w_op = sb("w_op", [P, C])
        negmax = sb("negmax", [P, NT, 2, 2])
        rowsum = sb("rowsum", [P, NT, 2, 2])
        lowest = sb("lowest", [P, NT, 2])
        shift = sb("shift", [P, NT, 2, 2])
        factor = sb("factor", [P, NT, 2, 2])
        part = sb("part", [P, NT, 2, 2])
        total = sb("total", [P, NT, 2])
        inverse = sb("inverse", [P, NT, 2])
        scales = sb("scales", [P, NT, 2, 2])
        wg_n = sb("wg_n", [P, 3, C])
        wu_n = sb("wu_n", [P, 3, C])
        wd_n = sb("wd_n", [C, FF])
        wgu_T = sb("wgu_T", [C, 2, FF])
        wd_T = sb("wd_T", [P, 3, C])
        zn = [sb(f"zn{k}", [P, GT, C]) for k in range(3)]
        zq = [sb(f"zq{k}", [P, GT, C]) for k in range(2)]
        gate_s = [sb(f"gate_s{k}", [P, GT, FF]) for k in range(2)]
        hid = sb("hid", [P, GT, FF])
        hq = [sb(f"hq{k}", [P, GT, FF]) for k in range(2)]
        qa = sb("qa", [P, GT * FF])
        qb = sb("qb", [P, GT * FF])
        qc = sb("qc", [P, GT * FF])
        amax = sb("amax", [P, 64])
        qscale = sb("qscale", [P, 64])
        qinv = sb("qinv", [P, 64])
        stats = sb("stats", [P, 2 * NG, GT, 6])
        mv = sb("mv", [P, 2 * NG, GT, 2])
        veps = sb("veps", [P, 2 * NG, GT])
        rstd = sb("rstd", [P, 2 * NG, GT])
        neg_half = sb("neg_half", [P, GT])
        z2 = [sb(f"z2{k}", [P, GT, C]) for k in range(2)]
        res = [sb(f"res{k}", [P, GT, C]) for k in range(2)]

        slots = [psum(f"slot{b}", [P, 2, BANK]) for b in range(2)]
        tp = [psum(f"tp{b}", [P, 2, GQ]) for b in range(2)]
        y_ps = psum("y_ps", [P, BANK])
        o_ps = psum("o_ps", [P, BANK])

        x_loaded = sem("x_loaded")
        wd_loaded = sem("wd_loaded")
        wqk_loaded = sem("wqk_loaded")
        wv_loaded = sem("wv_loaded")
        wo_loaded = sem("wo_loaded")
        ffw_loaded = sem("ffw_loaded")
        consts_made = sem("consts_made")
        consts_cast = sem("consts_cast")
        slot_filled = sem("slot_filled")
        slot_free = [sem(f"slot_free{b}") for b in range(2)]
        max_ready = sem("max_ready")
        high_ready = sem("high_ready")
        stacks_loaded = sem("stacks_loaded")
        stat_step = sem("stat_step")
        shift_ready = sem("shift_ready")
        factor_ready = sem("factor_ready")
        scales_ready = sem("scales_ready")
        rows_begun = sem("rows_begun")
        rows_scaled = sem("rows_scaled")
        turn_filled = sem("turn_filled")
        turn_copied = [sem(f"turn_copied{k}") for k in range(3)]
        y_filled = sem("y_filled")
        y_copied = sem("y_copied")
        o_filled = sem("o_filled")
        o_added = sem("o_added")
        ff_step = sem("ff_step")
        var_ready = sem("var_ready")
        rstd_ready = sem("rstd_ready")
        zq_ready = sem("zq_ready")
        silu_ready = sem("silu_ready")
        hq_ready = sem("hq_ready")
        wq_ready = sem("wq_ready")
        res_ready = sem("res_ready")
        stored = [sem(f"stored{k}") for k in range(2)]

        def slot_at(p, n):
            return p * SLOTS + (HEAD_SLOTS + n)

        def free_at(p, n):
            return p * (SLOTS // 2) + (HEAD_SLOTS // 2 + n // 2)

        def turns_copied(p, n):
            if n < 0:
                return p * (TURNS // 3) + ((n + TURNS) // 3 - TURNS // 3 + 2)
            return p * (TURNS // 3) + (n // 3 + 2)

        def ys_copied(p, n):
            return p * NG + (n + 1)

        def os_added(p, n):
            return p * NG + (n + 1)

        block = ctx.enter_context(nc.Block())

        @block.sync
        def _(sp):
            for k in range(2):
                sp.dma_start(resid[:, k * 8:(k + 1) * 8, :], x_t[:, k * 8:(k + 1) * 8, :]).then_inc(x_loaded, 16)
            sp.dma_start(w_d[:, :], w_kv_down).then_inc(wd_loaded, 16)

            def load_qk(p):
                sp.dma_start(w_qp[:, :], w_q[:, bass.ds(p * P, P)]).then_inc(wqk_loaded, 16)
                sp.dma_start(w_kp[:, :], w_kv_up[:, bass.ds(p * P, P)]).then_inc(wqk_loaded, 16)

            def load_v(p):
                sp.dma_start(w_vp[:, :], w_kv_up[:, bass.ds(p * P + HD, P)]).then_inc(wv_loaded, 16)

            def load_o(p):
                sp.dma_start(w_op[:, :], w_out[bass.ds(p * P, P), :]).then_inc(wo_loaded, 16)

            def move_halves(w, s, b, uses):
                sp.wait_ge(slot_free[b], uses)
                cols = slice(s * CH, (s + 1) * CH)
                up, down = slice(0, HEAD), slice(HEAD, P)
                if w == "q":
                    moves = [(q_st[0], down, q_lo, up), (q_st[1], up, q_lo, down)]
                else:
                    moves = [(k_st[0], down, k_sw[0], up), (k_sw[0], down, k_st[0], up),
                             (k_st[1], up, k_sw[1], down), (k_sw[1], up, k_st[1], down)]
                for to, a, frm, b in moves:
                    sp.dma_start(to[a, cols].bitcast(F32), frm[b, cols].bitcast(F32)).then_inc(stacks_loaded, 16)

            load_qk(0)
            load_v(0)
            load_o(0)
            sp.dma_start(wg_n[:, 0:2, :], w_gate[0:256, :].rearrange("(n p) c -> p n c", p=P)).then_inc(ffw_loaded, 16)
            sp.dma_start(wg_n[0:96, 2, :], w_gate[256:FF, :]).then_inc(ffw_loaded, 16)
            sp.dma_start(wu_n[:, 0:2, :], w_up[0:256, :].rearrange("(n p) c -> p n c", p=P)).then_inc(ffw_loaded, 16)
            sp.dma_start(wu_n[0:96, 2, :], w_up[256:FF, :]).then_inc(ffw_loaded, 16)
            sp.dma_start(wd_n[:, :], w_down).then_inc(ffw_loaded, 16)
            for w in "qk":
                for s in range(2):
                    move_halves(w, s, s, {"q": 3, "k": 4}[w])

            def body(p):
                sp.wait_ge(slot_filled, slot_at(p, 0))
                load_qk(p + 1)
                sp.wait_ge(slot_filled, slot_at(p, 2))
                load_v(p + 1)
                for it in pair:
                    if it[0] == "P":
                        move_halves(it[1], it[2], SLOT[it] % 2, free_at(p, SLOT[it]) + 1)
                sp.wait_ge(o_filled, p * NG + NG)
                load_o(p + 1)

            with sp.Fori(0, LAST) as p:
                body(p)
            for g in range(NG):
                sp.wait_ge(res_ready, g + 1)
                sp.dma_start(out_t[:, g * GT:(g + 1) * GT, :], res[g % 2][:, :, :]).then_inc(stored[g % 2], 16)
            for k in range(2):
                sp.wait_ge(stored[k], 16 * (NG // 2))

        @block.gpsimd
        def _(pool):
            pool.memset(ident[:, :], 0.0).then_inc(consts_made, 1)
            pool.memset(mask[:, :], 0.0).then_inc(consts_made, 1)
            pool.memset(neg_half[:, :], -0.5).then_inc(consts_made, 1)
            pool.wait_ge(consts_made, 3)
            pool.affine_select(out=ident[:, :], in_=ident[:, :], compare_op=ALU.not_equal, fill=1.0, base=0,
                               pattern=[[-1, P]], channel_multiplier=1).then_inc(consts_made, 1)
            pool.affine_select(out=mask[:, :], in_=mask[:, :], compare_op=ALU.is_ge, fill=MASKED, base=0,
                               pattern=[[-1, P]], channel_multiplier=1).then_inc(consts_made, 1)

            def scale_rows(p, i):
                pool.wait_ge(scales_ready, p * NT + i + 1)
                pool.sem_inc(rows_begun, 1)
                buf = probs[(i // GT) % 2]
                for c, (a, n) in enumerate(chunks(i)):
                    for h in range(2):
                        row = buf[:, i % GT, h, a:a + n]
                        pool.tensor_scalar(row, row, scales[:, i, h, c:c + 1], 1.0, ALU.mult,
                                           ALU.mult).then_inc(rows_scaled, 1)

            def rsqrt(k):
                pool.wait_ge(var_ready, k + 1)
                pool.tensor_tensor(rstd[:, k, :], veps[:, k, :], neg_half[:, :], ALU.pow).then_inc(rstd_ready, 1)

            def body(p, plan):
                norms = 0
                for it in plan:
                    if it[0] == "N":
                        scale_rows(p, it[1])
                    elif it[0] in ("FA", "FE"):
                        rsqrt(norms)
                        norms += 1

            with pool.Fori(0, LAST) as p:
                body(p, pair)
            body(LAST, final)

        @block.scalar
        def _(act):
            def xT_copy(s):
                act.wait_ge(slot_filled, s + 1)
                act.copy(xT[:, s * CH:(s + 1) * CH], slots[s % 2][:, :, :]).then_inc(slot_free[s % 2], 1)

            def latent_copy(s):
                act.wait_ge(slot_filled, 2 + s + 1)
                act.copy(latT[:, s * CH:(s + 1) * CH], slots[s % 2][:, :, :]).then_inc(slot_free[s % 2], 1)

            def high_parts(p, w, s, filled, b):
                act.wait_ge(slot_filled, filled + 1)
                stack = q_st if w == "q" else k_st
                scale = SCALE if w == "q" else 1.0
                cols = slice(s * CH, (s + 1) * CH)
                for h in range(2):
                    rows = slice(h * HEAD, (h + 1) * HEAD)
                    act.activation(stack[h][rows, cols], slots[b][rows, :, :], ACT.Copy,
                                   scale=scale).then_inc(high_ready, 1)

            def values(p, s):
                act.wait_ge(slot_filled, slot_at(p, s) + 1)
                act.copy(v[:, s * 8:(s + 1) * 8, :], slots[s % 2][:, :, :]).then_inc(slot_free[s % 2], 1)

            def exp_chunk(p, it, n, k):
                _, i, h, c = it
                a, width = chunks(i)[c]
                act.wait_ge(max_ready, p * CHUNKS + k + 1)
                act.activation(probs[(i // GT) % 2][:, i % GT, h, a:a + width],
                               slots[n % 2][:, :, :].rearrange("p a b -> p (a b)")[:, 0:width], ACT.Exp,
                               bias=negmax[:, i, h, c:c + 1], scale=1.0,
                               accum_out=rowsum[:, i, h, c:c + 1]).then_inc(slot_free[n % 2], 1)

            def factors(p, i):
                act.wait_ge(shift_ready, p * len(TWO) + TWO.index(i) + 1)
                act.activation(factor[:, i, :, :], shift[:, i, :, :], ACT.Exp).then_inc(factor_ready, 1)

            def turn_copy(p, g, j, n):
                act.wait_ge(turn_filled, p * TURNS + n + 1)
                lo = 0 if j <= GT * g else P
                act.copy(turned[n % 3][:, :, lo:GQ], tp[n % 2][:, :, lo:GQ]).then_inc(turn_copied[n % 3], 1)

            def y_copy(p, g):
                act.wait_ge(y_filled, p * NG + g + 1)
                act.copy(yT[g % 2][:, :], y_ps[:, 0:GQ]).then_inc(y_copied, 1)

            def body(p, plan, slot, turn, chunk):
                for it in plan:
                    if it[0] == "V":
                        values(p, it[1])
                    elif it[0] == "S":
                        exp_chunk(p, it, slot[it], chunk[it])
                    elif it[0] == "N" and it[1] in TWO:
                        factors(p, it[1])
                    elif it[0] == "T" and turn[it[1:]] % 3 != 2:
                        turn_copy(p, it[1], it[2], turn[it[1:]])
                    elif it[0] == "Y":
                        y_copy(p, it[1])
                    elif it[0] == "P":
                        high_parts(p + 1, it[1], it[2], slot_at(p, slot[it]), slot[it] % 2)
                    elif it[0] == "FB":
                        feed_gate(p, it[1])
                    elif it[0] == "FD":
                        feed_turned(p, it[1])

            def feed_gate(p, g):
                n = FTURN[("x", g)]
                act.wait_ge(turn_filled, p * TURNS + n + 1)
                act.copy(turned[n % 3][:, 0, :], tp[n % 2][:, 0, :]).then_inc(turn_copied[n % 3], 1)
                for t in range(GT):
                    m = FSLOT[("F", g, t)]
                    act.wait_ge(slot_filled, slot_at(p, m) + 1)
                    act.activation(gate_s[g % 2][:, t, :], slots[m % 2][:, 0, 0:FF],
                                   ACT.Silu).then_inc(silu_ready, 1)

            def feed_turned(p, g):
                for t in range(GT):
                    n = FTURN[("h", g, t)]
                    flat = turned[n % 3][:, :, :].rearrange("p a b -> p (a b)")
                    bank = tp[n % 2][:, :, :].rearrange("p a b -> p (a b)")
                    act.wait_ge(turn_filled, p * TURNS + n + 1)
                    act.copy(flat[:, 0:256], bank[:, 0:256])
                    act.copy(flat[0:96, 256:384], bank[0:96, 256:384]).then_inc(turn_copied[n % 3], 1)

            act.sem_inc(turn_copied[0], 1)
            act.sem_inc(turn_copied[1], 1)
            act.sem_inc(y_copied, 1)
            xT_copy(0)
            xT_copy(1)
            latent_copy(0)
            latent_copy(1)
            for w in "qk":
                for s in range(2):
                    high_parts(0, w, s, 4 + {"q": 0, "k": 2}[w] + s, s)
            with act.Fori(0, LAST) as p:
                body(p, pair, SLOT, TURN, CHUNK)
            body(LAST, final, FSLOT, FTURN, FCHUNK)

        @block.vector
        def _(dve):
            dve.wait_ge(consts_made, 5)
            dve.tensor_copy(ident_b[:, :], ident[:, :]).then_inc(consts_cast, 1)
            dve.tensor_copy(mask_b[:, :], mask[:, :]).then_inc(consts_cast, 1)
            dve.sem_inc(turn_copied[2], 1)
            dve.sem_inc(o_added, 1)
            steps = [0]

            def step(ins):
                ins.then_inc(ff_step, 1)
                steps[0] += 1
                dve.wait_ge(ff_step, steps[0])

            def low_parts(p, w, s, b):
                n = {"q": 0, "k": 2}[w] + s
                cols = slice(s * CH, (s + 1) * CH)
                scale = SCALE if w == "q" else 1.0
                stack = q_st if w == "q" else k_st
                dve.wait_ge(high_ready, p * 8 + 2 * n + 2)
                ps = slots[b][:, :, :].rearrange("p a b -> p (a b)")
                for h in range(2):
                    rows = slice(h * HEAD, (h + 1) * HEAD)
                    to = q_lo if w == "q" else k_sw[h]
                    ins = dve.scalar_tensor_tensor(out=to[rows, cols], in0=ps[rows, :], scalar=scale,
                                                   in1=stack[h][rows, cols].bitcast(F32),
                                                   op0=ALU.mult, op1=ALU.subtract)
                ins.then_inc(slot_free[b], 1)

            def chunk_max(p, it, n):
                _, i, h, c = it
                width = chunks(i)[c][1]
                dve.wait_ge(slot_filled, slot_at(p, n) + 1)
                dve.tensor_reduce(negmax[:, i, h, c:c + 1],
                                  slots[n % 2][:, :, :].rearrange("p a b -> p (a b)")[:, 0:width],
                                  AX.X, ALU.max, negate=True).then_inc(max_ready, 1)

            def shifts(p, i, k):
                base = p * (4 * len(TWO)) + 4 * TWO.index(i)
                dve.wait_ge(max_ready, p * CHUNKS + k + 1)
                dve.tensor_reduce(lowest[:, i, :], negmax[:, i, :, :], AX.X, ALU.min).then_inc(stat_step, 1)
                dve.wait_ge(stat_step, base + 1)
                dve.tensor_tensor(shift[:, i, :, :], lowest[:, i, :].unsqueeze(2).to_broadcast([P, 2, 2]),
                                  negmax[:, i, :, :], ALU.subtract).then_inc(shift_ready, 1)

            def row_scales(p, i, n):
                base = p * (4 * len(TWO))
                if i not in TWO:
                    dve.wait_ge(slot_free[n % 2], free_at(p, n) + 1)
                    dve.reciprocal(scales[:, i, :, 0], rowsum[:, i, :, 0]).then_inc(scales_ready, 1)
                    return
                base = base + 4 * TWO.index(i)
                dve.wait_ge(factor_ready, p * len(TWO) + TWO.index(i) + 1)
                dve.tensor_tensor(part[:, i, :, :], factor[:, i, :, :], rowsum[:, i, :, :],
                                  ALU.mult).then_inc(stat_step, 1)
                dve.wait_ge(stat_step, base + 2)
                dve.tensor_reduce(total[:, i, :], part[:, i, :, :], AX.X, ALU.add).then_inc(stat_step, 1)
                dve.wait_ge(stat_step, base + 3)
                dve.reciprocal(inverse[:, i, :], total[:, i, :]).then_inc(stat_step, 1)
                dve.wait_ge(stat_step, base + 4)
                dve.tensor_tensor(scales[:, i, :, :], factor[:, i, :, :],
                                  inverse[:, i, :].unsqueeze(2).to_broadcast([P, 2, 2]),
                                  ALU.mult).then_inc(scales_ready, 1)

            def turn_copy(p, g, j, n):
                dve.wait_ge(turn_filled, p * TURNS + n + 1)
                lo = 0 if j <= GT * g else P
                dve.tensor_copy(turned[n % 3][:, :, lo:GQ], tp[n % 2][:, :, lo:GQ]).then_inc(turn_copied[n % 3], 1)

            def add_output(p, g):
                dve.wait_ge(o_filled, p * NG + g + 1)
                dst = resid[:, g * GT:(g + 1) * GT, :].rearrange("p a b -> p (a b)")
                dve.tensor_tensor(dst, o_ps[:, 0:GQ], dst, ALU.add).then_inc(o_added, 1)

            def quantise(src, dst, n, ready, rows=P):
                nb = n // BLK
                def blocks(t):
                    return t[0:rows, 0:n].rearrange("p (b k) -> p b k", k=BLK)
                def spread(t):
                    return t[0:rows, 0:nb].unsqueeze(2).to_broadcast([rows, nb, BLK])
                s3 = src.rearrange("p (b k) -> p b k", k=BLK)
                step(dve.tensor_reduce(amax[0:rows, 0:nb], s3, AX.X, ALU.max, apply_absolute_value=True))
                step(dve.tensor_scalar(qscale[0:rows, 0:nb], amax[0:rows, 0:nb], 1.0 / FP4_MAX, 1e-12,
                                       ALU.mult, ALU.max))
                step(dve.reciprocal(amax[0:rows, 0:nb], qscale[0:rows, 0:nb]))
                step(dve.tensor_scalar(qinv[0:rows, 0:nb], amax[0:rows, 0:nb], BELOW_ONE, None, ALU.mult))
                step(dve.tensor_tensor(blocks(qa), s3, spread(qinv), ALU.mult))
                a, b, c = (t[0:rows, 0:n] for t in (qa, qb, qc))
                step(dve.tensor_scalar(a.bitcast(U32), a.bitcast(U32), 0x7FFFFFFF, None, ALU.bitwise_and))
                step(dve.tensor_scalar(b, a, 2.0, 4.0, ALU.max, ALU.min))
                step(dve.tensor_scalar(b, b, ONE_MAGIC, ONE_MAGIC, ALU.add, ALU.subtract))
                step(dve.tensor_scalar(c, a, 2.0, HALF_MAGIC, ALU.min, ALU.add))
                step(dve.scalar_tensor_tensor(out=b, in0=c, scalar=HALF_MAGIC, in1=b,
                                              op0=ALU.subtract, op1=ALU.add))
                step(dve.tensor_scalar(c, a, 4.0, TWO_MAGIC, ALU.max, ALU.add))
                step(dve.scalar_tensor_tensor(out=b, in0=c, scalar=TWO_MAGIC + 6.0, in1=b,
                                              op0=ALU.subtract, op1=ALU.add))
                step(dve.tensor_tensor(blocks(qa), blocks(qb), spread(qscale), ALU.mult))
                dve.scalar_tensor_tensor(out=dst.bitcast(U32), in0=src.bitcast(U32), scalar=0x80000000,
                                         in1=a.bitcast(U32), op0=ALU.bitwise_and,
                                         op1=ALU.bitwise_or).then_inc(ready, 1)

            def layer_norm(src, dst, k, last):
                for t in range(GT):
                    step(dve.bn_stats(stats[:, k, t, :], src[:, t, :]))
                    step(dve.bn_aggr(mv[:, k, t, :], stats[:, k, t, :]))
                dve.tensor_scalar(veps[:, k, :], mv[:, k, :, 1], EPS, None, ALU.add).then_inc(var_ready, 1)
                dve.wait_ge(rstd_ready, k + 1)
                for t in range(GT):
                    ins = dve.tensor_scalar(dst[:, t, :], src[:, t, :], mv[:, k, t, 0:1], rstd[:, k, t:t + 1],
                                            ALU.subtract, ALU.mult)
                    if t < GT - 1 or last is None:
                        step(ins)
                    else:
                        ins.then_inc(last, 1)

            def flat(t):
                return t.rearrange("p a b -> p (a b)")

            def feed_weights(p):
                dve.wait_ge(ffw_loaded, 16 * 5)
                for nat in (wg_n, wu_n):
                    for k, (a, n) in enumerate(FFK):
                        quantise(nat[0:n, k, :], nat[0:n, k, :], C, wq_ready, rows=n)
                        qstep[0] += 1
                        dve.wait_ge(wq_ready, qstep[0])
                quantise(wd_n[:, :], wd_n[:, :], FF, wq_ready)
                qstep[0] += 1
                dve.wait_ge(wq_ready, qstep[0])
                for w in range(3):
                    n = FTURN[("w", w)]
                    bank = flat(tp[n % 2][:, :, :])
                    dve.wait_ge(turn_filled, p * TURNS + n + 1)
                    if w < 2:
                        dve.tensor_copy(wgu_T[:, w, :], bank[:, 0:FF]).then_inc(turn_copied[n % 3], 1)
                    else:
                        step(dve.tensor_copy(flat(wd_T[:, 0:2, :]), bank[:, 0:256]))
                        dve.tensor_copy(wd_T[0:96, 2, :], bank[0:96, 256:384]).then_inc(turn_copied[n % 3], 1)

            qstep = [0]

            def feed_input(g, k):
                layer_norm(resid[:, g * GT:(g + 1) * GT, :], zn[g % 3], k, None)
                quantise(flat(zn[g % 3][:, :, :]), flat(zq[g % 2][:, :, :]), GT * C, zq_ready)
                dve.wait_ge(zq_ready, g + 1)

            def feed_hidden(p, g):
                for t in range(GT):
                    m = FSLOT[("F", g, t)]
                    dve.wait_ge(silu_ready, GT * g + t + 1)
                    dve.tensor_tensor(hid[:, t, :], slots[m % 2][:, 1, 0:FF], gate_s[g % 2][:, t, :],
                                      ALU.mult).then_inc(slot_free[m % 2], 1)
                for t in range(GT):
                    m = FSLOT[("F", g, t)]
                    dve.wait_ge(slot_free[m % 2], free_at(p, m) + 1)
                quantise(flat(hid[:, :, :]), flat(hq[g % 2][:, :, :]), GT * FF, hq_ready)
                dve.wait_ge(hq_ready, g + 1)

            def feed_output(p, g, k):
                dve.wait_ge(o_filled, p * NG + NG + g + 1)
                dve.tensor_tensor(flat(z2[g % 2][:, :, :]), o_ps[:, 0:GQ], flat(zn[g % 3][:, :, :]),
                                  ALU.add).then_inc(o_added, 1)
                dve.wait_ge(o_added, os_added(p, NG + g + 1))
                if g >= 2:
                    dve.wait_ge(stored[g % 2], 16 * (g // 2))
                layer_norm(z2[g % 2], res[g % 2], k, res_ready)

            def body(p, plan, slot, turn, chunk):
                norms = 0
                for n_it, it in enumerate(plan):
                    if it[0] == "S":
                        chunk_max(p, it, slot[it])
                    elif it[0] == "N":
                        i = it[1]
                        s = ("S", i, 1, len(chunks(i)) - 1)
                        if i in TWO:
                            shifts(p, i, chunk[s])
                        row_scales(p, i, slot[s])
                    elif it[0] == "T" and turn[it[1:]] % 3 == 2:
                        turn_copy(p, it[1], it[2], turn[it[1:]])
                    elif it[0] == "O":
                        add_output(p, it[1])
                    elif it[0] == "P":
                        low_parts(p + 1, it[1], it[2], slot[it] % 2)
                    elif it[0] == "FW":
                        feed_weights(p)
                    elif it[0] == "FA":
                        feed_input(it[1], norms)
                        norms += 1
                    elif it[0] == "FH":
                        feed_hidden(p, it[1])
                    elif it[0] == "FE":
                        feed_output(p, it[1], norms)
                        norms += 1

            for w in "qk":
                for s in range(2):
                    low_parts(0, w, s, s)
            with dve.Fori(0, LAST) as p:
                body(p, pair, SLOT, TURN, CHUNK)
            body(LAST, final, FSLOT, FTURN, FCHUNK)

        @block.tensor
        def _(pe):
            def slot_reusable(p, n):
                pe.wait_ge(slot_free[n % 2], free_at(p, n))

            def project(w, s, b, lhs, rhs):
                for k in range(2):
                    a = s * CH + k * BANK
                    ins = pe.matmul(slots[b][:, k, :], lhs[:, :], rhs[:, a:a + BANK], start=True, stop=True)
                ins.then_inc(slot_filled, 1)

            def values(p, s, n):
                slot_reusable(p, n)
                pe.wait_ge(wv_loaded, (p + 1) * 16)
                for t in range(8):
                    j = s * 8 + t
                    ins = pe.matmul(slots[n % 2][:, t // 4, (t % 4) * P:(t % 4 + 1) * P],
                                    latT[:, j * P:(j + 1) * P], w_vp[:, :], start=True, stop=True)
                ins.then_inc(slot_filled, 1)

            def scores(p, it, n):
                _, i, h, c = it
                a, width = chunks(i)[c]
                slot_reusable(p, n)
                diag = a + width == (i + 1) * P
                q = q_st[h][:, i * P:(i + 1) * P]
                for b in range(0, width, BANK):
                    m = min(BANK, width - b)
                    end = diag and b + m == width
                    dst = slots[n % 2][:, b // BANK, 0:m]
                    keys = slice(a + b, a + b + m)
                    pe.matmul(dst, q, k_st[h][:, keys], start=True, stop=False)
                    ins = pe.matmul(dst, q, k_sw[h][:, keys], start=False, stop=not end)
                    if end:
                        ins = pe.matmul(slots[n % 2][:, b // BANK, m - P:m], ident_b[:, :], mask_b[:, :],
                                        start=False, stop=True)
                ins.then_inc(slot_filled, 1)

            def turn(p, g, j, n, scaled):
                pe.wait_ge(turn_copied[(n - 2) % 3], turns_copied(p, n - 2))
                i = GT * g + GT - 1
                pe.wait_ge(rows_scaled, p * NORMS + scaled[(i, 1, j * P // CH)])
                lo = 0 if j <= GT * g else 1
                for h in range(2):
                    for t in range(lo, GT):
                        ins = pe.transpose(tp[n % 2][:, h, t * P:(t + 1) * P],
                                           probs[g % 2][:, t, h, j * P:(j + 1) * P], ident[:, :])
                ins.then_inc(turn_filled, 1)

            def times_values(p, g, j, n):
                pe.wait_ge(turn_copied[n % 3], turns_copied(p, n))
                last = GT * g + GT - 1
                lo = 0 if j <= GT * g else P
                for h in range(2):
                    ins = pe.matmul(y_ps[h * HEAD:(h + 1) * HEAD, lo:GQ], v[:, j, h * HEAD:(h + 1) * HEAD],
                                    turned[n % 3][:, h, lo:GQ], start=(j == 0), stop=(j == last))
                if j == last:
                    ins.then_inc(y_filled, 1)

            def project_out(p, g):
                pe.wait_ge(y_copied, ys_copied(p, g + 1))
                pe.wait_ge(o_added, os_added(p, g))
                pe.wait_ge(wo_loaded, (p + 1) * 16)
                for t in range(GT):
                    ins = pe.matmul(o_ps[:, t * P:(t + 1) * P], yT[g % 2][:, t * P:(t + 1) * P], w_op[:, :],
                                    start=True, stop=True)
                ins.then_inc(o_filled, 1)

            def bank_free(p, n):
                pe.wait_ge(turn_copied[(n - 2) % 3], turns_copied(p, n - 2))

            def feed_weights(p):
                pe.wait_ge(wq_ready, 7)
                for w in range(3):
                    n = FTURN[("w", w)]
                    bank_free(p, n)
                    bank = tp[n % 2][:, :, :].rearrange("p a b -> p (a b)")
                    for k, (a, m) in enumerate(FFK):
                        if w < 2:
                            nat = (wg_n, wu_n)[w]
                            ins = pe.transpose(bank[:, a:a + m], nat[0:m, k, :], ident[0:m, 0:m])
                        else:
                            ins = pe.transpose(bank[0:m, k * P:(k + 1) * P], wd_n[:, a:a + m], ident[:, :])
                    ins.then_inc(turn_filled, 1)

            def feed_up(p, g):
                n = FTURN[("x", g)]
                bank_free(p, n)
                pe.wait_ge(zq_ready, g + 1)
                for t in range(GT):
                    ins = pe.transpose(tp[n % 2][:, 0, t * P:(t + 1) * P], zq[g % 2][:, t, :], ident[:, :])
                ins.then_inc(turn_filled, 1)
                pe.wait_ge(turn_copied[n % 3], turns_copied(p, n))
                for t in range(GT):
                    m = FSLOT[("F", g, t)]
                    slot_reusable(p, m)
                    for k in range(2):
                        ins = pe.matmul(slots[m % 2][:, k, 0:FF], turned[n % 3][:, 0, t * P:(t + 1) * P],
                                        wgu_T[:, k, :], start=True, stop=True)
                    ins.then_inc(slot_filled, 1)

            def feed_down(p, g):
                pe.wait_ge(hq_ready, g + 1)
                for t in range(GT):
                    n = FTURN[("h", g, t)]
                    bank_free(p, n)
                    bank = tp[n % 2][:, :, :].rearrange("p a b -> p (a b)")
                    for k, (a, m) in enumerate(FFK):
                        ins = pe.transpose(bank[0:m, k * P:(k + 1) * P], hq[g % 2][:, t, a:a + m], ident[:, :])
                    ins.then_inc(turn_filled, 1)
                pe.wait_ge(o_added, os_added(p, NG + g))
                for t in range(GT):
                    n = FTURN[("h", g, t)]
                    pe.wait_ge(turn_copied[n % 3], turns_copied(p, n))
                    flat = turned[n % 3][:, :, :].rearrange("p a b -> p (a b)")
                    for k, (a, m) in enumerate(FFK):
                        ins = pe.matmul(o_ps[:, t * P:(t + 1) * P], flat[0:m, k * P:(k + 1) * P],
                                        wd_T[0:m, k, :], start=(k == 0), stop=(k == 2))
                ins.then_inc(o_filled, 1)

            def body(p, plan, slot, turns, scaled):
                for it in plan:
                    if it[0] == "V":
                        values(p, it[1], slot[it])
                    elif it[0] == "S":
                        if it[1:] == (0, 0, 0):
                            pe.wait_ge(stacks_loaded, (p + 1) * (16 * 12))
                        scores(p, it, slot[it])
                    elif it[0] == "T":
                        g, j = it[1:]
                        turn(p, g, j, turns[(g, j)], scaled)
                        if j == 1 and g == 0:
                            pe.wait_ge(slot_free[1], free_at(p, 1) + 1)
                        if j == 1:
                            pe.wait_ge(y_copied, ys_copied(p, g))
                        if j:
                            times_values(p, g, j - 1, turns[(g, j - 1)])
                    elif it[0] == "Y":
                        j = GT * it[1] + GT - 1
                        times_values(p, it[1], j, turns[(it[1], j)])
                    elif it[0] == "O":
                        project_out(p, it[1])
                    elif it[0] == "P":
                        slot_reusable(p, slot[it])
                        if it[1:] == ("q", 0):
                            pe.wait_ge(wqk_loaded, (p + 2) * 32)
                        w, rhs = (w_qp, xT) if it[1] == "q" else (w_kp, latT)
                        project(it[1], it[2], slot[it] % 2, w, rhs)
                    elif it[0] == "FW":
                        feed_weights(p)
                    elif it[0] == "FB":
                        feed_up(p, it[1])
                    elif it[0] == "FD":
                        feed_down(p, it[1])

            pe.wait_ge(consts_made, 5)
            for s in range(2):
                pe.wait_ge(x_loaded, 32)
                for t in range(8):
                    ins = pe.transpose(slots[s][:, t // 4, (t % 4) * P:(t % 4 + 1) * P], resid[:, s * 8 + t, :],
                                       ident[:, :])
                ins.then_inc(slot_filled, 1)
            pe.wait_ge(wd_loaded, 16)
            for s in range(2):
                pe.wait_ge(slot_free[s], 1)
                project("l", s, s, w_d, xT)
            pe.wait_ge(wqk_loaded, 32)
            for s in range(2):
                pe.wait_ge(slot_free[s], 2)
                project("q", s, s, w_qp, xT)
            for s in range(2):
                pe.wait_ge(slot_free[s], 3)
                project("k", s, s, w_kp, latT)
            pe.wait_ge(consts_cast, 2)
            with pe.Fori(0, LAST) as p:
                body(p, pair, SLOT, TURN, SCALED)
            body(LAST, final, FSLOT, FTURN, FSCALED)


_INS = ["L0_attn_x", "L0_attn_w_kv_down", "L0_attn_w_kv_up", "L0_attn_w_q", "L0_attn_w_out",
        "L0_ffn_w_gate", "L0_ffn_w_up", "L0_ffn_w_down"]
_OUTS = [((1, 2048, 128), "float32")]


def kernel(**inputs):
    import numpy as _np
    import concourse.bacc as _bacc
    from concourse import mybir as _mybir
    from concourse.bass_utils import run_bass_kernel_spmd as _run

    nc = _bacc.Bacc("TRN2", target_bir_lowering=False, num_devices=1)
    arrays, args = {}, []
    for name in _INS:
        a = _np.ascontiguousarray(inputs[name])
        arrays[f"in_{name}_dram"] = a
        args.append(nc.dram_tensor(f"in_{name}_dram", a.shape, _mybir.dt.from_np(a.dtype), kind="ExternalInput").ap())
    for i, (shape, dtype) in enumerate(_OUTS):
        dt = _mybir.dt.from_np(_np.dtype(dtype))
        args.append(nc.dram_tensor(f"out_{i}_dram", shape, dt, kind="ExternalOutput").ap())
    block_kernel(nc, *args)
    r = _run(nc, [arrays], core_ids=[0])
    got = tuple(r.results[0][f"out_{i}_dram"] for i in range(len(_OUTS)))
    return got[0]
```

```python
import concourse.bass as bass
from concourse import mybir
from contextlib import ExitStack

F32 = mybir.dt.float32
F32R = mybir.dt.float32r
BF16 = mybir.dt.bfloat16
U32 = mybir.dt.uint32
ALU = mybir.AluOpType
ACT = mybir.ActivationFunctionType
AX = mybir.AxisListType

P = 128
T = 2048
C = 128
NT = T // P
HEADS, HEAD = 16, 64
HD = HEADS * HEAD
PAIRS = HEADS // 2
SCALE = HEAD ** -0.5
GT = 2
NG = NT // GT
GQ = GT * P
CH = 1024
BANK = 512
FF = 352
BLK = 16
FFK = [(0, 128), (128, 128), (256, 96)]
EPS = 1e-5
MASKED = -3.0e38
FP4_MAX = 6.0
HALF_MAGIC = 1.5 * 2 ** 22
ONE_MAGIC = 1.5 * 2 ** 23
TWO_MAGIC = 1.5 * 2 ** 24
BELOW_ONE = 1.0 - 2.0 ** -23


def chunks(i):
    width = (i + 1) * P
    return [(a, min(CH, width - a)) for a in range(0, width, CH)]


def row_slots(i):
    out = []
    for c, (a, n) in enumerate(chunks(i)):
        out += [((0, c), (1, c))] if n <= BANK else [((0, c),), ((1, c),)]
    return out


LAG = 3
TURN_AGE, OUT_AGE = 3, 3


def pair_plan(last):
    plan, waiting = [], []

    def take():
        item = waiting.pop(0)[1]
        plan.append(item)
        if item[0] == "M" and item[2] == GT * item[1] + GT - 1:
            waiting.insert(0, [0, ("O", item[1])])

    def put(it):
        while it[0] == "T" and sum(w[1][0] == "M" for w in waiting) > 2:
            take()
        plan.append(it)
        grown = {"T": 1, "S": 2, "V": 2, "P": 2}.get(it[0], 0)
        for w in waiting:
            w[0] += grown
        if it[0] == "T":
            waiting.append([0, ("M",) + it[1:]])
        while waiting and waiting[0][0] >= (TURN_AGE if waiting[0][1][0] == "M" else OUT_AGE):
            take()

    put(("V", 0))
    put(("V", 1))
    turns, norm = [], None
    for g in range(NG):
        slots = []
        for i in range(GT * g, GT * (g + 1)):
            for k, parts in enumerate(row_slots(i)):
                slots.append(("S", i, parts))
                if k == 0 and norm is not None:
                    slots.append(("N", norm))
            norm = i
        n = sum(s[0] == "S" for s in slots)
        lag = min(LAG, n - 1)
        k = done = 0
        for s in slots:
            put(s)
            k += s[0] == "S"
            want = len(turns) * max(0, k - lag) // (n - lag)
            while done < want:
                put(turns[done])
                done += 1
        turns = [("T", g, j) for j in range(GT * g + GT)]
    tail = [] if last else [("P", "q", 0), ("P", "q", 1), ("P", "k", 0), ("P", "k", 1)]
    for t in tail[:1] + [("N", NT - 1)] + tail[1:]:
        put(t)
    for t in turns:
        put(t)
    while waiting:
        take()
    return plan


def ffn_plan():
    plan = [("FW",)]
    for k in range(NG + 2):
        plan += [("FA", k), ("FB", k)] if k < NG else []
        plan += [("FH", k - 1), ("FD", k - 1)] if 0 < k <= NG else []
        plan += [("FE", k - 2)] if k >= 2 else []
    return plan


def numbers(plan):
    slot, turn, chunk, scaled = {}, {}, {}, {}
    ns = nt = nc_ = nn = 0
    for it in plan:
        if it[0] in ("V", "S", "P"):
            slot[it] = ns
            ns += 1
        if it[0] == "S":
            chunk[it] = nc_
            nc_ += 1
        if it[0] == "T":
            turn[it[1:]] = nt
            nt += 1
        if it[0] == "N":
            for c in range(len(chunks(it[1]))):
                for h in range(2):
                    nn += 1
                    scaled[(it[1], h, c)] = nn
        if it[0] == "FB":
            for t in range(GT):
                slot[("F", it[1], t)] = ns
                ns += 1
            turn[("x", it[1])] = nt
            nt += 1
        if it[0] == "FD":
            for t in range(GT):
                turn[("h", it[1], t)] = nt
                nt += 1
        if it[0] == "FW":
            for w in range(3):
                turn[("w", w)] = nt
                nt += 1
    return slot, turn, chunk, scaled


def block_kernel(nc, x, w_kv_down, w_kv_up, w_q, w_out, w_gate, w_up, w_down, out):
    pair = pair_plan(False)
    final = pair_plan(True) + ffn_plan()
    SLOT, TURN, CHUNK, SCALED = numbers(pair)
    FSLOT, FTURN, FCHUNK, FSCALED = numbers(final)
    HEAD_SLOTS = 8
    CHUNKS = sum(len(row_slots(i)) for i in range(NT))
    SLOTS = 2 + CHUNKS + 4
    TURNS = sum(GT * g + GT for g in range(NG))
    assert SLOTS % 2 == 0 and TURNS % 3 == 0
    NORMS = sum(2 * len(chunks(i)) for i in range(NT))
    TWO = [i for i in range(NT) if len(chunks(i)) == 2]
    LAST = PAIRS - 1

    x_t = x.rearrange("a (n p) c -> p (a n) c", p=P)
    out_t = out.rearrange("a (n p) c -> p (a n) c", p=P)

    with ExitStack() as ctx:
        def sb(name, shape, dt=F32):
            return ctx.enter_context(nc.sbuf_tensor(name, shape, dt))

        def psum(name, shape, dt=F32):
            return ctx.enter_context(nc.psum_tensor(name, shape, dt))

        def sem(name):
            return ctx.enter_context(nc.semaphore(name))

        resid = sb("resid", [P, NT, C])
        xT = sb("xT", [C, T])
        latT = sb("latT", [C, T])
        q_st = [sb(f"q_st{h}", [P, T], F32R) for h in range(2)]
        k_st = [sb(f"k_st{h}", [P, T], F32R) for h in range(2)]
        k_sw = [sb(f"k_sw{h}", [P, T], F32R) for h in range(2)]
        q_lo = sb("q_lo", [P, T], F32R)
        v = sb("v", [P, NT, P])
        probs = [sb(f"probs{k}", [P, GT, 2, T]) for k in range(2)]
        turned = [sb(f"turned{k}", [P, 2, GQ]) for k in range(3)]
        yT = [sb(f"yT{k}", [P, GQ]) for k in range(2)]
        ident = sb("ident", [P, P])
        ident_b = sb("ident_b", [P, P], BF16)
        mask = sb("mask", [P, P])
        mask_b = sb("mask_b", [P, P], BF16)
        w_d = sb("w_d", [C, C])
        w_qp = sb("w_qp", [C, P])
        w_kp = sb("w_kp", [C, P])
        w_vp = sb("w_vp", [C, P])
        w_op = sb("w_op", [P, C])
        negmax = sb("negmax", [P, NT, 2, 2])
        rowsum = sb("rowsum", [P, NT, 2, 2])
        lowest = sb("lowest", [P, NT, 2])
        shift = sb("shift", [P, NT, 2, 2])
        factor = sb("factor", [P, NT, 2, 2])
        part = sb("part", [P, NT, 2, 2])
        total = sb("total", [P, NT, 2])
        inverse = sb("inverse", [P, NT, 2])
        scales = sb("scales", [P, NT, 2, 2])
        wg_n = sb("wg_n", [P, 3, C])
        wu_n = sb("wu_n", [P, 3, C])
        wd_n = sb("wd_n", [C, FF])
        wgu_T = sb("wgu_T", [C, 2, FF])
        wd_T = sb("wd_T", [P, 3, C])
        zn = [sb(f"zn{k}", [P, GT, C]) for k in range(3)]
        zq = [sb(f"zq{k}", [P, GT, C]) for k in range(2)]
        gate_s = [sb(f"gate_s{k}", [P, GT, FF]) for k in range(2)]
        hid = sb("hid", [P, GT, FF])
        hq = [sb(f"hq{k}", [P, GT, FF]) for k in range(2)]
        qa = sb("qa", [P, GT * FF])
        qb = sb("qb", [P, GT * FF])
        qc = sb("qc", [P, GT * FF])
        amax = sb("amax", [P, 64])
        qscale = sb("qscale", [P, 64])
        qinv = sb("qinv", [P, 64])
        stats = sb("stats", [P, 2 * NG, GT, 6])
        mv = sb("mv", [P, 2 * NG, GT, 2])
        veps = sb("veps", [P, 2 * NG, GT])
        rstd = sb("rstd", [P, 2 * NG, GT])
        neg_half = sb("neg_half", [P, GT])
        z2 = [sb(f"z2{k}", [P, GT, C]) for k in range(2)]
        res = [sb(f"res{k}", [P, GT, C]) for k in range(2)]

        slots = [psum(f"slot{b}", [P, 2, BANK]) for b in range(2)]
        tp = [psum(f"tp{b}", [P, 2, GQ]) for b in range(3)]
        yo_ps = psum("yo_ps", [P, 2, GQ])
        y_ps, o_ps = yo_ps[:, 0, :], yo_ps[:, 1, :]

        x_loaded = sem("x_loaded")
        wd_loaded = sem("wd_loaded")
        wqk_loaded = sem("wqk_loaded")
        wv_loaded = sem("wv_loaded")
        wo_loaded = sem("wo_loaded")
        ffw_loaded = sem("ffw_loaded")
        consts_made = sem("consts_made")
        consts_cast = sem("consts_cast")
        slot_filled = sem("slot_filled")
        slot_free = [sem(f"slot_free{b}") for b in range(2)]
        max_ready = sem("max_ready")
        high_ready = sem("high_ready")
        stacks_loaded = sem("stacks_loaded")
        stat_step = sem("stat_step")
        shift_ready = sem("shift_ready")
        factor_ready = sem("factor_ready")
        scales_ready = sem("scales_ready")
        rows_begun = sem("rows_begun")
        rows_scaled = sem("rows_scaled")
        turn_filled = sem("turn_filled")
        turn_copied = [sem(f"turn_copied{k}") for k in range(3)]
        y_filled = sem("y_filled")
        y_copied = sem("y_copied")
        o_filled = sem("o_filled")
        o_added = sem("o_added")
        ff_step = sem("ff_step")
        var_ready = sem("var_ready")
        rstd_ready = sem("rstd_ready")
        zq_ready = sem("zq_ready")
        silu_ready = sem("silu_ready")
        hq_ready = sem("hq_ready")
        wq_ready = sem("wq_ready")
        res_ready = sem("res_ready")
        stored = [sem(f"stored{k}") for k in range(2)]

        def slot_at(p, n):
            return p * SLOTS + (HEAD_SLOTS + n)

        def free_at(p, n):
            return p * (SLOTS // 2) + (HEAD_SLOTS // 2 + n // 2)

        def turns_copied(p, n):
            if n < 0:
                return p * (TURNS // 3) + ((n + TURNS) // 3 - TURNS // 3 + 2)
            return p * (TURNS // 3) + (n // 3 + 2)

        def ys_copied(p, n):
            return p * NG + (n + 1)

        def os_added(p, n):
            return p * NG + (n + 1)

        block = ctx.enter_context(nc.Block())

        @block.sync
        def _(sp):
            for k in range(2):
                sp.dma_start(resid[:, k * 8:(k + 1) * 8, :], x_t[:, k * 8:(k + 1) * 8, :]).then_inc(x_loaded, 16)
            sp.dma_start(w_d[:, :], w_kv_down).then_inc(wd_loaded, 16)

            def load_qk(p):
                sp.dma_start(w_qp[:, :], w_q[:, bass.ds(p * P, P)]).then_inc(wqk_loaded, 16)
                sp.dma_start(w_kp[:, :], w_kv_up[:, bass.ds(p * P, P)]).then_inc(wqk_loaded, 16)

            def load_v(p):
                sp.dma_start(w_vp[:, :], w_kv_up[:, bass.ds(p * P + HD, P)]).then_inc(wv_loaded, 16)

            def load_o(p):
                sp.dma_start(w_op[:, :], w_out[bass.ds(p * P, P), :]).then_inc(wo_loaded, 16)

            def move_halves(w, s, b, uses):
                sp.wait_ge(slot_free[b], uses)
                cols = slice(s * CH, (s + 1) * CH)
                up, down = slice(0, HEAD), slice(HEAD, P)
                if w == "q":
                    moves = [(q_st[0], down, q_lo, up), (q_st[1], up, q_lo, down)]
                else:
                    moves = [(k_st[0], down, k_sw[0], up), (k_sw[0], down, k_st[0], up),
                             (k_st[1], up, k_sw[1], down), (k_sw[1], up, k_st[1], down)]
                for to, a, frm, b in moves:
                    sp.dma_start(to[a, cols].bitcast(F32), frm[b, cols].bitcast(F32)).then_inc(stacks_loaded, 16)

            load_qk(0)
            load_v(0)
            load_o(0)
            sp.dma_start(wg_n[:, 0:2, :], w_gate[0:256, :].rearrange("(n p) c -> p n c", p=P)).then_inc(ffw_loaded, 16)
            sp.dma_start(wg_n[0:96, 2, :], w_gate[256:FF, :]).then_inc(ffw_loaded, 16)
            sp.dma_start(wu_n[:, 0:2, :], w_up[0:256, :].rearrange("(n p) c -> p n c", p=P)).then_inc(ffw_loaded, 16)
            sp.dma_start(wu_n[0:96, 2, :], w_up[256:FF, :]).then_inc(ffw_loaded, 16)
            sp.dma_start(wd_n[:, :], w_down).then_inc(ffw_loaded, 16)
            for w in "qk":
                for s in range(2):
                    move_halves(w, s, s, {"q": 3, "k": 4}[w])

            def body(p):
                sp.wait_ge(slot_filled, slot_at(p, 0))
                load_qk(p + 1)
                sp.wait_ge(slot_filled, slot_at(p, 2))
                load_v(p + 1)
                for it in pair:
                    if it[0] == "P":
                        move_halves(it[1], it[2], SLOT[it] % 2, free_at(p, SLOT[it]) + 1)
                sp.wait_ge(o_filled, p * NG + NG)
                load_o(p + 1)

            with sp.Fori(0, LAST) as p:
                body(p)
            for g in range(NG):
                sp.wait_ge(res_ready, g + 1)
                sp.dma_start(out_t[:, g * GT:(g + 1) * GT, :], res[g % 2][:, :, :]).then_inc(stored[g % 2], 16)
            for k in range(2):
                sp.wait_ge(stored[k], 16 * (NG // 2))

        @block.gpsimd
        def _(pool):
            pool.memset(ident[:, :], 0.0).then_inc(consts_made, 1)
            pool.memset(mask[:, :], 0.0).then_inc(consts_made, 1)
            pool.memset(neg_half[:, :], -0.5).then_inc(consts_made, 1)
            pool.wait_ge(consts_made, 3)
            pool.affine_select(out=ident[:, :], in_=ident[:, :], compare_op=ALU.not_equal, fill=1.0, base=0,
                               pattern=[[-1, P]], channel_multiplier=1).then_inc(consts_made, 1)
            pool.affine_select(out=mask[:, :], in_=mask[:, :], compare_op=ALU.is_ge, fill=MASKED, base=0,
                               pattern=[[-1, P]], channel_multiplier=1).then_inc(consts_made, 1)

            def scale_rows(p, i):
                pool.wait_ge(scales_ready, p * NT + i + 1)
                pool.sem_inc(rows_begun, 1)
                buf = probs[(i // GT) % 2]
                for c, (a, n) in enumerate(chunks(i)):
                    for h in range(2):
                        row = buf[:, i % GT, h, a:a + n]
                        pool.tensor_scalar(row, row, scales[:, i, h, c:c + 1], 1.0, ALU.mult,
                                           ALU.mult).then_inc(rows_scaled, 1)

            def rsqrt(k):
                pool.wait_ge(var_ready, k + 1)
                pool.tensor_tensor(rstd[:, k, :], veps[:, k, :], neg_half[:, :], ALU.pow).then_inc(rstd_ready, 1)

            def body(p, plan):
                norms = 0
                for it in plan:
                    if it[0] == "N":
                        scale_rows(p, it[1])
                    elif it[0] in ("FA", "FE"):
                        rsqrt(norms)
                        norms += 1

            with pool.Fori(0, LAST) as p:
                body(p, pair)
            body(LAST, final)

        @block.scalar
        def _(act):
            def xT_copy(s):
                act.wait_ge(slot_filled, s + 1)
                act.copy(xT[:, s * CH:(s + 1) * CH], slots[s % 2][:, :, :]).then_inc(slot_free[s % 2], 1)

            def latent_copy(s):
                act.wait_ge(slot_filled, 2 + s + 1)
                act.copy(latT[:, s * CH:(s + 1) * CH], slots[s % 2][:, :, :]).then_inc(slot_free[s % 2], 1)

            def high_parts(p, w, s, filled, b):
                act.wait_ge(slot_filled, filled + 1)
                stack = q_st if w == "q" else k_st
                scale = SCALE if w == "q" else 1.0
                cols = slice(s * CH, (s + 1) * CH)
                for h in range(2):
                    rows = slice(h * HEAD, (h + 1) * HEAD)
                    act.activation(stack[h][rows, cols], slots[b][rows, :, :], ACT.Copy,
                                   scale=scale).then_inc(high_ready, 1)

            def values(p, s):
                act.wait_ge(slot_filled, slot_at(p, s) + 1)
                act.copy(v[:, s * 8:(s + 1) * 8, :], slots[s % 2][:, :, :]).then_inc(slot_free[s % 2], 1)

            def exp_chunk(p, it, n, k):
                _, i, parts = it
                act.wait_ge(max_ready, p * CHUNKS + k + 1)
                for b, (h, c) in enumerate(parts):
                    a, width = chunks(i)[c]
                    scores = slots[n % 2][:, b:, :].rearrange("p a b -> p (a b)")[:, 0:width]
                    ins = act.activation(probs[(i // GT) % 2][:, i % GT, h, a:a + width], scores, ACT.Exp,
                                         bias=negmax[:, i, h, c:c + 1], scale=1.0,
                                         accum_out=rowsum[:, i, h, c:c + 1])
                ins.then_inc(slot_free[n % 2], 1)

            def factors(p, i):
                act.wait_ge(shift_ready, p * len(TWO) + TWO.index(i) + 1)
                act.activation(factor[:, i, :, :], shift[:, i, :, :], ACT.Exp).then_inc(factor_ready, 1)

            def turn_copy(p, g, j, n):
                act.wait_ge(turn_filled, p * TURNS + n + 1)
                lo = 0 if j <= GT * g else P
                act.copy(turned[n % 3][:, :, lo:GQ], tp[n % 3][:, :, lo:GQ]).then_inc(turn_copied[n % 3], 1)

            def y_copy(p, g):
                act.wait_ge(y_filled, p * NG + g + 1)
                act.copy(yT[g % 2][:, :], y_ps).then_inc(y_copied, 1)

            def body(p, plan, slot, turn, chunk):
                for it in plan:
                    if it[0] == "V":
                        values(p, it[1])
                    elif it[0] == "S":
                        exp_chunk(p, it, slot[it], chunk[it])
                    elif it[0] == "N" and it[1] in TWO:
                        factors(p, it[1])
                    elif it[0] == "T" and turn[it[1:]] % 3 != 2:
                        turn_copy(p, it[1], it[2], turn[it[1:]])
                    elif it[0] == "M" and it[2] == GT * it[1] + GT - 1:
                        y_copy(p, it[1])
                    elif it[0] == "P":
                        high_parts(p + 1, it[1], it[2], slot_at(p, slot[it]), slot[it] % 2)
                    elif it[0] == "FB":
                        feed_gate(p, it[1])
                    elif it[0] == "FD":
                        feed_turned(p, it[1])

            def feed_gate(p, g):
                n = FTURN[("x", g)]
                act.wait_ge(turn_filled, p * TURNS + n + 1)
                act.copy(turned[n % 3][:, 0, :], tp[n % 3][:, 0, :]).then_inc(turn_copied[n % 3], 1)
                for t in range(GT):
                    m = FSLOT[("F", g, t)]
                    act.wait_ge(slot_filled, slot_at(p, m) + 1)
                    act.activation(gate_s[g % 2][:, t, :], slots[m % 2][:, 0, 0:FF],
                                   ACT.Silu).then_inc(silu_ready, 1)

            def feed_turned(p, g):
                for t in range(GT):
                    n = FTURN[("h", g, t)]
                    flat = turned[n % 3][:, :, :].rearrange("p a b -> p (a b)")
                    bank = tp[n % 3][:, :, :].rearrange("p a b -> p (a b)")
                    act.wait_ge(turn_filled, p * TURNS + n + 1)
                    act.copy(flat[:, 0:256], bank[:, 0:256])
                    act.copy(flat[0:96, 256:384], bank[0:96, 256:384]).then_inc(turn_copied[n % 3], 1)

            act.sem_inc(turn_copied[0], 1)
            act.sem_inc(turn_copied[1], 1)
            act.sem_inc(y_copied, 1)
            xT_copy(0)
            xT_copy(1)
            latent_copy(0)
            latent_copy(1)
            for w in "qk":
                for s in range(2):
                    high_parts(0, w, s, 4 + {"q": 0, "k": 2}[w] + s, s)
            with act.Fori(0, LAST) as p:
                body(p, pair, SLOT, TURN, CHUNK)
            body(LAST, final, FSLOT, FTURN, FCHUNK)

        @block.vector
        def _(dve):
            dve.wait_ge(consts_made, 5)
            dve.tensor_copy(ident_b[:, :], ident[:, :]).then_inc(consts_cast, 1)
            dve.tensor_copy(mask_b[:, :], mask[:, :]).then_inc(consts_cast, 1)
            dve.sem_inc(turn_copied[2], 1)
            dve.sem_inc(o_added, 1)
            steps = [0]

            def step(ins):
                ins.then_inc(ff_step, 1)
                steps[0] += 1
                dve.wait_ge(ff_step, steps[0])

            def low_parts(p, w, s, b):
                n = {"q": 0, "k": 2}[w] + s
                cols = slice(s * CH, (s + 1) * CH)
                scale = SCALE if w == "q" else 1.0
                stack = q_st if w == "q" else k_st
                dve.wait_ge(high_ready, p * 8 + 2 * n + 2)
                ps = slots[b][:, :, :].rearrange("p a b -> p (a b)")
                for h in range(2):
                    rows = slice(h * HEAD, (h + 1) * HEAD)
                    to = q_lo if w == "q" else k_sw[h]
                    ins = dve.scalar_tensor_tensor(out=to[rows, cols], in0=ps[rows, :], scalar=scale,
                                                   in1=stack[h][rows, cols].bitcast(F32),
                                                   op0=ALU.mult, op1=ALU.subtract)
                ins.then_inc(slot_free[b], 1)

            def chunk_max(p, it, n):
                _, i, parts = it
                h, c = parts[0]
                width = chunks(i)[c][1]
                dve.wait_ge(slot_filled, slot_at(p, n) + 1)
                if len(parts) == 2:
                    to, frm = negmax[:, i, :, c], slots[n % 2][:, :, 0:width]
                else:
                    to = negmax[:, i, h, c:c + 1]
                    frm = slots[n % 2][:, :, :].rearrange("p a b -> p (a b)")[:, 0:width]
                dve.tensor_reduce(to, frm, AX.X, ALU.max, negate=True).then_inc(max_ready, 1)

            def shifts(p, i, k):
                base = p * (4 * len(TWO)) + 4 * TWO.index(i)
                dve.wait_ge(max_ready, p * CHUNKS + k + 1)
                dve.tensor_reduce(lowest[:, i, :], negmax[:, i, :, :], AX.X, ALU.min).then_inc(stat_step, 1)
                dve.wait_ge(stat_step, base + 1)
                dve.tensor_tensor(shift[:, i, :, :], lowest[:, i, :].unsqueeze(2).to_broadcast([P, 2, 2]),
                                  negmax[:, i, :, :], ALU.subtract).then_inc(shift_ready, 1)

            def row_scales(p, i, n):
                base = p * (4 * len(TWO))
                if i not in TWO:
                    dve.wait_ge(slot_free[n % 2], free_at(p, n) + 1)
                    dve.reciprocal(scales[:, i, :, 0], rowsum[:, i, :, 0]).then_inc(scales_ready, 1)
                    return
                base = base + 4 * TWO.index(i)
                dve.wait_ge(factor_ready, p * len(TWO) + TWO.index(i) + 1)
                dve.tensor_tensor(part[:, i, :, :], factor[:, i, :, :], rowsum[:, i, :, :],
                                  ALU.mult).then_inc(stat_step, 1)
                dve.wait_ge(stat_step, base + 2)
                dve.tensor_reduce(total[:, i, :], part[:, i, :, :], AX.X, ALU.add).then_inc(stat_step, 1)
                dve.wait_ge(stat_step, base + 3)
                dve.reciprocal(inverse[:, i, :], total[:, i, :]).then_inc(stat_step, 1)
                dve.wait_ge(stat_step, base + 4)
                dve.tensor_tensor(scales[:, i, :, :], factor[:, i, :, :],
                                  inverse[:, i, :].unsqueeze(2).to_broadcast([P, 2, 2]),
                                  ALU.mult).then_inc(scales_ready, 1)

            def turn_copy(p, g, j, n):
                dve.wait_ge(turn_filled, p * TURNS + n + 1)
                lo = 0 if j <= GT * g else P
                dve.tensor_copy(turned[n % 3][:, :, lo:GQ], tp[n % 3][:, :, lo:GQ]).then_inc(turn_copied[n % 3], 1)

            def add_output(p, g):
                dve.wait_ge(o_filled, p * NG + g + 1)
                dst = resid[:, g * GT:(g + 1) * GT, :].rearrange("p a b -> p (a b)")
                dve.tensor_tensor(dst, o_ps, dst, ALU.add).then_inc(o_added, 1)

            def quantise(src, dst, n, ready, rows=P):
                nb = n // BLK
                def blocks(t):
                    return t[0:rows, 0:n].rearrange("p (b k) -> p b k", k=BLK)
                def spread(t):
                    return t[0:rows, 0:nb].unsqueeze(2).to_broadcast([rows, nb, BLK])
                s3 = src.rearrange("p (b k) -> p b k", k=BLK)
                step(dve.tensor_reduce(amax[0:rows, 0:nb], s3, AX.X, ALU.max, apply_absolute_value=True))
                step(dve.tensor_scalar(qscale[0:rows, 0:nb], amax[0:rows, 0:nb], 1.0 / FP4_MAX, 1e-12,
                                       ALU.mult, ALU.max))
                step(dve.reciprocal(amax[0:rows, 0:nb], qscale[0:rows, 0:nb]))
                step(dve.tensor_scalar(qinv[0:rows, 0:nb], amax[0:rows, 0:nb], BELOW_ONE, None, ALU.mult))
                step(dve.tensor_tensor(blocks(qa), s3, spread(qinv), ALU.mult))
                a, b, c = (t[0:rows, 0:n] for t in (qa, qb, qc))
                step(dve.tensor_scalar(a.bitcast(U32), a.bitcast(U32), 0x7FFFFFFF, None, ALU.bitwise_and))
                step(dve.tensor_scalar(b, a, 2.0, 4.0, ALU.max, ALU.min))
                step(dve.tensor_scalar(b, b, ONE_MAGIC, ONE_MAGIC, ALU.add, ALU.subtract))
                step(dve.tensor_scalar(c, a, 2.0, HALF_MAGIC, ALU.min, ALU.add))
                step(dve.scalar_tensor_tensor(out=b, in0=c, scalar=HALF_MAGIC, in1=b,
                                              op0=ALU.subtract, op1=ALU.add))
                step(dve.tensor_scalar(c, a, 4.0, TWO_MAGIC, ALU.max, ALU.add))
                step(dve.scalar_tensor_tensor(out=b, in0=c, scalar=TWO_MAGIC + 6.0, in1=b,
                                              op0=ALU.subtract, op1=ALU.add))
                step(dve.tensor_tensor(blocks(qa), blocks(qb), spread(qscale), ALU.mult))
                dve.scalar_tensor_tensor(out=dst.bitcast(U32), in0=src.bitcast(U32), scalar=0x80000000,
                                         in1=a.bitcast(U32), op0=ALU.bitwise_and,
                                         op1=ALU.bitwise_or).then_inc(ready, 1)

            def layer_norm(src, dst, k, last):
                for t in range(GT):
                    step(dve.bn_stats(stats[:, k, t, :], src[:, t, :]))
                    step(dve.bn_aggr(mv[:, k, t, :], stats[:, k, t, :]))
                dve.tensor_scalar(veps[:, k, :], mv[:, k, :, 1], EPS, None, ALU.add).then_inc(var_ready, 1)
                dve.wait_ge(rstd_ready, k + 1)
                for t in range(GT):
                    ins = dve.tensor_scalar(dst[:, t, :], src[:, t, :], mv[:, k, t, 0:1], rstd[:, k, t:t + 1],
                                            ALU.subtract, ALU.mult)
                    if t < GT - 1 or last is None:
                        step(ins)
                    else:
                        ins.then_inc(last, 1)

            def flat(t):
                return t.rearrange("p a b -> p (a b)")

            def feed_weights(p):
                dve.wait_ge(ffw_loaded, 16 * 5)
                for nat in (wg_n, wu_n):
                    for k, (a, n) in enumerate(FFK):
                        quantise(nat[0:n, k, :], nat[0:n, k, :], C, wq_ready, rows=n)
                        qstep[0] += 1
                        dve.wait_ge(wq_ready, qstep[0])
                quantise(wd_n[:, :], wd_n[:, :], FF, wq_ready)
                qstep[0] += 1
                dve.wait_ge(wq_ready, qstep[0])
                for w in range(3):
                    n = FTURN[("w", w)]
                    bank = flat(tp[n % 3][:, :, :])
                    dve.wait_ge(turn_filled, p * TURNS + n + 1)
                    if w < 2:
                        dve.tensor_copy(wgu_T[:, w, :], bank[:, 0:FF]).then_inc(turn_copied[n % 3], 1)
                    else:
                        step(dve.tensor_copy(flat(wd_T[:, 0:2, :]), bank[:, 0:256]))
                        dve.tensor_copy(wd_T[0:96, 2, :], bank[0:96, 256:384]).then_inc(turn_copied[n % 3], 1)

            qstep = [0]

            def feed_input(g, k):
                layer_norm(resid[:, g * GT:(g + 1) * GT, :], zn[g % 3], k, None)
                quantise(flat(zn[g % 3][:, :, :]), flat(zq[g % 2][:, :, :]), GT * C, zq_ready)
                dve.wait_ge(zq_ready, g + 1)

            def feed_hidden(p, g):
                for t in range(GT):
                    m = FSLOT[("F", g, t)]
                    dve.wait_ge(silu_ready, GT * g + t + 1)
                    dve.tensor_tensor(hid[:, t, :], slots[m % 2][:, 1, 0:FF], gate_s[g % 2][:, t, :],
                                      ALU.mult).then_inc(slot_free[m % 2], 1)
                for t in range(GT):
                    m = FSLOT[("F", g, t)]
                    dve.wait_ge(slot_free[m % 2], free_at(p, m) + 1)
                quantise(flat(hid[:, :, :]), flat(hq[g % 2][:, :, :]), GT * FF, hq_ready)
                dve.wait_ge(hq_ready, g + 1)

            def feed_output(p, g, k):
                dve.wait_ge(o_filled, p * NG + NG + g + 1)
                dve.tensor_tensor(flat(z2[g % 2][:, :, :]), o_ps, flat(zn[g % 3][:, :, :]),
                                  ALU.add).then_inc(o_added, 1)
                dve.wait_ge(o_added, os_added(p, NG + g + 1))
                if g >= 2:
                    dve.wait_ge(stored[g % 2], 16 * (g // 2))
                layer_norm(z2[g % 2], res[g % 2], k, res_ready)

            def body(p, plan, slot, turn, chunk):
                norms = 0
                for n_it, it in enumerate(plan):
                    if it[0] == "S":
                        chunk_max(p, it, slot[it])
                    elif it[0] == "N":
                        i = it[1]
                        s = ("S", i, row_slots(i)[-1])
                        if i in TWO:
                            shifts(p, i, chunk[s])
                        row_scales(p, i, slot[s])
                    elif it[0] == "T" and turn[it[1:]] % 3 == 2:
                        turn_copy(p, it[1], it[2], turn[it[1:]])
                    elif it[0] == "O":
                        add_output(p, it[1])
                    elif it[0] == "P":
                        low_parts(p + 1, it[1], it[2], slot[it] % 2)
                    elif it[0] == "FW":
                        feed_weights(p)
                    elif it[0] == "FA":
                        feed_input(it[1], norms)
                        norms += 1
                    elif it[0] == "FH":
                        feed_hidden(p, it[1])
                    elif it[0] == "FE":
                        feed_output(p, it[1], norms)
                        norms += 1

            for w in "qk":
                for s in range(2):
                    low_parts(0, w, s, s)
            with dve.Fori(0, LAST) as p:
                body(p, pair, SLOT, TURN, CHUNK)
            body(LAST, final, FSLOT, FTURN, FCHUNK)

        @block.tensor
        def _(pe):
            def slot_reusable(p, n):
                pe.wait_ge(slot_free[n % 2], free_at(p, n))

            def project(w, s, b, lhs, rhs):
                for k in range(2):
                    a = s * CH + k * BANK
                    ins = pe.matmul(slots[b][:, k, :], lhs[:, :], rhs[:, a:a + BANK], start=True, stop=True)
                ins.then_inc(slot_filled, 1)

            def values(p, s, n):
                slot_reusable(p, n)
                pe.wait_ge(wv_loaded, (p + 1) * 16)
                for t in range(8):
                    j = s * 8 + t
                    ins = pe.matmul(slots[n % 2][:, t // 4, (t % 4) * P:(t % 4 + 1) * P],
                                    latT[:, j * P:(j + 1) * P], w_vp[:, :], start=True, stop=True)
                ins.then_inc(slot_filled, 1)

            def scores(p, it, n):
                _, i, parts = it
                slot_reusable(p, n)
                for bank, (h, c) in enumerate(parts):
                    a, width = chunks(i)[c]
                    q = q_st[h][:, i * P:(i + 1) * P]
                    for b in range(0, width, BANK):
                        m = min(BANK, width - b)
                        end = a + b + m == (i + 1) * P
                        at = bank + b // BANK
                        keys = slice(a + b, a + b + m)
                        pe.matmul(slots[n % 2][:, at, 0:m], q, k_st[h][:, keys], start=True, stop=False)
                        ins = pe.matmul(slots[n % 2][:, at, 0:m], q, k_sw[h][:, keys], start=False, stop=not end)
                        if end:
                            ins = pe.matmul(slots[n % 2][:, at, m - P:m], ident_b[:, :], mask_b[:, :],
                                            start=False, stop=True)
                ins.then_inc(slot_filled, 1)

            def turn(p, g, j, n, scaled):
                pe.wait_ge(turn_copied[n % 3], turns_copied(p, n - 3))
                i = GT * g + GT - 1
                pe.wait_ge(rows_scaled, p * NORMS + scaled[(i, 1, j * P // CH)])
                lo = 0 if j <= GT * g else 1
                for h in range(2):
                    for t in range(lo, GT):
                        ins = pe.transpose(tp[n % 3][:, h, t * P:(t + 1) * P],
                                           probs[g % 2][:, t, h, j * P:(j + 1) * P], ident[:, :])
                ins.then_inc(turn_filled, 1)

            def times_values(p, g, j, n):
                pe.wait_ge(turn_copied[n % 3], turns_copied(p, n))
                last = GT * g + GT - 1
                lo = 0 if j <= GT * g else P
                for h in range(2):
                    ins = pe.matmul(y_ps[h * HEAD:(h + 1) * HEAD, lo:GQ], v[:, j, h * HEAD:(h + 1) * HEAD],
                                    turned[n % 3][:, h, lo:GQ], start=(j == 0), stop=(j == last))
                if j == last:
                    ins.then_inc(y_filled, 1)

            def project_out(p, g):
                pe.wait_ge(y_copied, ys_copied(p, g + 1))
                pe.wait_ge(wo_loaded, (p + 1) * 16)
                for t in range(GT):
                    ins = pe.matmul(o_ps[:, t * P:(t + 1) * P], yT[g % 2][:, t * P:(t + 1) * P], w_op[:, :],
                                    start=True, stop=True)
                ins.then_inc(o_filled, 1)

            def bank_free(p, n):
                pe.wait_ge(turn_copied[n % 3], turns_copied(p, n - 3))

            def feed_weights(p):
                pe.wait_ge(wq_ready, 7)
                for w in range(3):
                    n = FTURN[("w", w)]
                    bank_free(p, n)
                    bank = tp[n % 3][:, :, :].rearrange("p a b -> p (a b)")
                    for k, (a, m) in enumerate(FFK):
                        if w < 2:
                            nat = (wg_n, wu_n)[w]
                            ins = pe.transpose(bank[:, a:a + m], nat[0:m, k, :], ident[0:m, 0:m])
                        else:
                            ins = pe.transpose(bank[0:m, k * P:(k + 1) * P], wd_n[:, a:a + m], ident[:, :])
                    ins.then_inc(turn_filled, 1)

            def feed_up(p, g):
                n = FTURN[("x", g)]
                bank_free(p, n)
                pe.wait_ge(zq_ready, g + 1)
                for t in range(GT):
                    ins = pe.transpose(tp[n % 3][:, 0, t * P:(t + 1) * P], zq[g % 2][:, t, :], ident[:, :])
                ins.then_inc(turn_filled, 1)
                pe.wait_ge(turn_copied[n % 3], turns_copied(p, n))
                for t in range(GT):
                    m = FSLOT[("F", g, t)]
                    slot_reusable(p, m)
                    for k in range(2):
                        ins = pe.matmul(slots[m % 2][:, k, 0:FF], turned[n % 3][:, 0, t * P:(t + 1) * P],
                                        wgu_T[:, k, :], start=True, stop=True)
                    ins.then_inc(slot_filled, 1)

            def feed_down(p, g):
                pe.wait_ge(hq_ready, g + 1)
                for t in range(GT):
                    n = FTURN[("h", g, t)]
                    bank_free(p, n)
                    bank = tp[n % 3][:, :, :].rearrange("p a b -> p (a b)")
                    for k, (a, m) in enumerate(FFK):
                        ins = pe.transpose(bank[0:m, k * P:(k + 1) * P], hq[g % 2][:, t, a:a + m], ident[:, :])
                    ins.then_inc(turn_filled, 1)
                pe.wait_ge(o_added, os_added(p, NG + g))
                for t in range(GT):
                    n = FTURN[("h", g, t)]
                    pe.wait_ge(turn_copied[n % 3], turns_copied(p, n))
                    flat = turned[n % 3][:, :, :].rearrange("p a b -> p (a b)")
                    for k, (a, m) in enumerate(FFK):
                        ins = pe.matmul(o_ps[:, t * P:(t + 1) * P], flat[0:m, k * P:(k + 1) * P],
                                        wd_T[0:m, k, :], start=(k == 0), stop=(k == 2))
                ins.then_inc(o_filled, 1)

            def body(p, plan, slot, turns, scaled):
                for it in plan:
                    if it[0] == "V":
                        values(p, it[1], slot[it])
                    elif it[0] == "S":
                        if it[1] == 0:
                            pe.wait_ge(stacks_loaded, (p + 1) * (16 * 12))
                        scores(p, it, slot[it])
                    elif it[0] == "T":
                        g, j = it[1:]
                        turn(p, g, j, turns[(g, j)], scaled)
                    elif it[0] == "M":
                        g, j = it[1:]
                        if j == 0:
                            pe.wait_ge(o_added, os_added(p, g))
                            if g == 0:
                                pe.wait_ge(slot_free[1], free_at(p, 1) + 1)
                        times_values(p, g, j, turns[(g, j)])
                    elif it[0] == "O":
                        project_out(p, it[1])
                    elif it[0] == "P":
                        slot_reusable(p, slot[it])
                        if it[1:] == ("q", 0):
                            pe.wait_ge(wqk_loaded, (p + 2) * 32)
                        w, rhs = (w_qp, xT) if it[1] == "q" else (w_kp, latT)
                        project(it[1], it[2], slot[it] % 2, w, rhs)
                    elif it[0] == "FW":
                        feed_weights(p)
                    elif it[0] == "FB":
                        feed_up(p, it[1])
                    elif it[0] == "FD":
                        feed_down(p, it[1])

            pe.wait_ge(consts_made, 5)
            for s in range(2):
                pe.wait_ge(x_loaded, 32)
                for t in range(8):
                    ins = pe.transpose(slots[s][:, t // 4, (t % 4) * P:(t % 4 + 1) * P], resid[:, s * 8 + t, :],
                                       ident[:, :])
                ins.then_inc(slot_filled, 1)
            pe.wait_ge(wd_loaded, 16)
            for s in range(2):
                pe.wait_ge(slot_free[s], 1)
                project("l", s, s, w_d, xT)
            pe.wait_ge(wqk_loaded, 32)
            for s in range(2):
                pe.wait_ge(slot_free[s], 2)
                project("q", s, s, w_qp, xT)
            for s in range(2):
                pe.wait_ge(slot_free[s], 3)
                project("k", s, s, w_kp, latT)
            pe.wait_ge(consts_cast, 2)
            with pe.Fori(0, LAST) as p:
                body(p, pair, SLOT, TURN, SCALED)
            body(LAST, final, FSLOT, FTURN, FSCALED)


_INS = ["L0_attn_x", "L0_attn_w_kv_down", "L0_attn_w_kv_up", "L0_attn_w_q", "L0_attn_w_out",
        "L0_ffn_w_gate", "L0_ffn_w_up", "L0_ffn_w_down"]
_OUTS = [((1, 2048, 128), "float32")]


def kernel(**inputs):
    import numpy as _np
    import concourse.bacc as _bacc
    from concourse import mybir as _mybir
    from concourse.bass_utils import run_bass_kernel_spmd as _run

    nc = _bacc.Bacc("TRN2", target_bir_lowering=False, num_devices=1)
    arrays, args = {}, []
    for name in _INS:
        a = _np.ascontiguousarray(inputs[name])
        arrays[f"in_{name}_dram"] = a
        args.append(nc.dram_tensor(f"in_{name}_dram", a.shape, _mybir.dt.from_np(a.dtype), kind="ExternalInput").ap())
    for i, (shape, dtype) in enumerate(_OUTS):
        dt = _mybir.dt.from_np(_np.dtype(dtype))
        args.append(nc.dram_tensor(f"out_{i}_dram", shape, dt, kind="ExternalOutput").ap())
    block_kernel(nc, *args)
    r = _run(nc, [arrays], core_ids=[0])
    got = tuple(r.results[0][f"out_{i}_dram"] for i in range(len(_OUTS)))
    return got[0]
```

```python
import concourse.bass as bass
from concourse import mybir
from contextlib import ExitStack

F32 = mybir.dt.float32
F32R = mybir.dt.float32r
BF16 = mybir.dt.bfloat16
U32 = mybir.dt.uint32
ALU = mybir.AluOpType
ACT = mybir.ActivationFunctionType
AX = mybir.AxisListType

P = 128
T = 2048
C = 128
NT = T // P
HEADS, HEAD = 16, 64
HD = HEADS * HEAD
PAIRS = HEADS // 2
SCALE = HEAD ** -0.5
GT = 2
NG = NT // GT
GQ = GT * P
CH = 1024
BANK = 512
FF = 352
BLK = 16
FFK = [(0, 128), (128, 128), (256, 96)]
EPS = 1e-5
MASKED = -3.0e38
FP4_MAX = 6.0
HALF_MAGIC = 1.5 * 2 ** 22
SPLITTER = 2.0 ** 22 + 1
BELOW_ONE = 1.0 - 2.0 ** -23


def chunks(i):
    width = (i + 1) * P
    return [(a, min(CH, width - a)) for a in range(0, width, CH)]


def row_slots(i):
    out = []
    for c, (a, n) in enumerate(chunks(i)):
        out += [((0, c), (1, c))] if n <= BANK else [((0, c),), ((1, c),)]
    return out


LAG = 2
TURN_AGE, OUT_AGE = 3, 3
FEED_S, FEED_T = 5, 3
ACT_LATE, DVE_LATE = 3, 0
FIRST_P, KEEP, P_AFTER = 6, 4, 4
PROJECTIONS = [("q", 0), ("k", 0), ("q", 1), ("k", 1)]
GAP = 4
QSTEPS = 10


def feed_chains():
    wait = [("gap",)] * GAP
    steps = []
    for g in range(NG + 1):
        first, second = [], []
        if g < NG:
            first += [("norm", 0, g, s) for s in range(3)] + wait + [("norm", 0, g, 3), ("abs", 0, g)]
            first += [("quant", 0, g, s) for s in range(QSTEPS)] + wait + [("turn", 0, g), ("product", g)]
        if g > 0:
            second += [("abs", 1, g - 1)] + [("quant", 1, g - 1, s) for s in range(QSTEPS)] + wait
            second += [("turn", 1, g - 1), ("sum", g - 1)] + [("norm", 1, g - 1, s) for s in range(3)]
            second += wait + [("norm", 1, g - 1, 3)]
        for k in range(max(len(first), len(second))):
            steps += first[k:k + 1] + second[k:k + 1]
    return steps


def pair_plan(last):
    plan = []
    waiting = []
    owed = []
    feed = feed_chains() if last else []
    turned = [0]

    def take():
        _, item, _ = waiting.pop(0)
        if item[0] in ("up", "down"):
            pay()
        plan.append(item)
        if item[0] == "M" and item[2] == GT * item[1] + GT - 1:
            waiting.insert(0, [0, ("O", item[1]), None])
        if item[0] == "up":
            owed.append(("product", item[1]))
        if item[0] == "down":
            owed.append(("sum", item[1]))

    def pay():
        while owed:
            plan.append(owed.pop(0))

    def turning():
        while any(w[2] is not None and w[2] <= turned[0] - 3 for w in waiting):
            take()
        turned[0] += 1

    def grow(n):
        for w in waiting:
            w[0] += n
        while waiting and waiting[0][0] >= (OUT_AGE if waiting[0][1][0] == "O" else TURN_AGE):
            take()

    def put(it):
        if it[0] in ("V", "S", "P"):
            pay()
        if it[0] == "T":
            turning()
        plan.append(it)
        grow({"T": 1, "S": 2, "V": 2, "P": 2}.get(it[0], 0))
        if it[0] == "T":
            waiting.append([0, ("M",) + it[1:], turned[0] - 1])
        feed_some({"T": FEED_T, "S": FEED_S}.get(it[0], 0), False)

    def feed_some(n, draining):
        for _ in range(n):
            if not feed:
                return
            it = feed[0]
            if it[:2] == ("norm", 0) and it[3] == 0 and ("O", it[2]) not in plan:
                return
            if it[0] in ("product", "sum"):
                reader = ({"product": "up", "sum": "down"}[it[0]], it[1])
                while draining and reader not in plan:
                    take()
                if reader not in plan:
                    return
                if it in owed:
                    pay()
                feed.pop(0)
                continue
            feed.pop(0)
            if it[0] == "gap":
                continue
            for _ in range(1 + it[1] if it[0] == "turn" else 0):
                turning()
            plan.append(it)
            if it[0] == "turn":
                grow(1 + it[1])
                waiting.append([0, (("up", "down")[it[1]], it[2]), turned[0] - 1 - it[1]])

    put(("V", 0))
    put(("V", 1))
    turns, norm = [], None
    parts_of = [] if last else [("P",) + w for w in PROJECTIONS]
    for g in range(NG):
        slots = []
        for i in range(GT * g, GT * (g + 1)):
            for k, parts in enumerate(row_slots(i)):
                slots.append(("S", i, parts))
                if k == len(row_slots(i)) - 1 and len(chunks(i)) == 2:
                    slots.append(("F", i))
                if k == 0 and norm is not None:
                    slots.append(("N", norm))
            norm = i
        n = sum(s[0] == "S" for s in slots)
        lag = min(LAG, n - 1)
        k = done = 0
        for s in slots:
            put(s)
            k += s[0] == "S"
            if s[0] == "S" and parts_of and g == FIRST_P and k == n - 2:
                put(parts_of.pop(0))
            most = len(turns) - (KEEP if g == NG - 1 else 0)
            want = most * max(0, k - lag) // (n - lag)
            while done < want:
                put(turns[done])
                done += 1
        left = turns[done:]
        turns = [("T", g, j) for j in range(GT * g + GT)]
    for t in parts_of[:1] + [("N", NT - 1)] + left + parts_of[1:2]:
        put(t)
    del parts_of[:2]
    for k, t in enumerate(turns):
        put(t)
        if parts_of and k >= P_AFTER:
            put(parts_of.pop(0))
    if last:
        while ("O", NG - 1) not in plan:
            take()
    while feed:
        feed_some(1, True)
    while waiting:
        take()
    pay()
    return plan


def later(plan, kind, turns):
    out, held, passed = [], [], 0
    for it in plan:
        if held and it[0] == "F":
            held.append(it)
            continue
        if held and (it[0] in ("S", "V", "P", "N", "up", "down", "product", "sum") or passed == turns):
            out += held
            held = []
        if it[0] == kind and turns:
            held, passed = [it], 0
            continue
        if it[0] == "T":
            passed += 1
        out.append(it)
    return out + held


def numbers(plan):
    slot, turn, chunk, scaled = {}, {}, {}, {}
    ns = nt = nc_ = nn = 0
    for it in plan:
        if it[0] in ("V", "S", "P"):
            slot[it] = ns
            ns += 1
        if it[0] == "S":
            chunk[it] = nc_
            nc_ += 1
        if it[0] == "T":
            turn[it[1:]] = nt
            nt += 1
        if it[0] == "N":
            for c in range(len(chunks(it[1]))):
                for h in range(2):
                    nn += 1
                    scaled[(it[1], h, c)] = nn
        if it[0] == "up":
            for t in range(GT):
                slot[it + (t,)] = ns
                ns += 1
        if it[0] == "down":
            slot[it] = ns
            ns += 1
        if it[0] == "turn":
            for t in range(1 + it[1]):
                turn[it + (t,)] = nt
                nt += 1
    return slot, turn, chunk, scaled


def block_kernel(nc, x, w_kv_down, w_kv_up, w_q, w_out, w_gate, w_up, w_down, out):
    pair = pair_plan(False)
    final = pair_plan(True)
    SLOT, TURN, CHUNK, SCALED = numbers(pair)
    FSLOT, FTURN, FCHUNK, FSCALED = numbers(final)
    HEAD_SLOTS = 10
    CHUNKS = sum(len(row_slots(i)) for i in range(NT))
    SLOTS = 2 + CHUNKS + 4
    TURNS = sum(GT * g + GT for g in range(NG))
    assert SLOTS % 2 == 0 and TURNS % 3 == 0
    NORMS = sum(2 * len(chunks(i)) for i in range(NT))
    TWO = [i for i in range(NT) if len(chunks(i)) == 2]
    LAST = PAIRS - 1

    x_t = x.rearrange("a (n p) c -> p (a n) c", p=P)
    out_t = out.rearrange("a (n p) c -> p (a n) c", p=P)

    with ExitStack() as ctx:
        def sb(name, shape, dt=F32):
            return ctx.enter_context(nc.sbuf_tensor(name, shape, dt))

        def psum(name, shape, dt=F32):
            return ctx.enter_context(nc.psum_tensor(name, shape, dt))

        def sem(name):
            return ctx.enter_context(nc.semaphore(name))

        resid = sb("resid", [P, NT, C])
        xT = sb("xT", [C, T])
        latT = sb("latT", [C, T])
        q_st = [sb(f"q_st{h}", [P, T], F32R) for h in range(2)]
        k_st = [sb(f"k_st{h}", [P, T], F32R) for h in range(2)]
        k_sw = [sb(f"k_sw{h}", [P, T], F32R) for h in range(2)]
        q_lo = sb("q_lo", [P, T], F32R)
        v = sb("v", [P, NT, P])
        probs = [sb(f"probs{k}", [P, GT, 2, T]) for k in range(2)]
        turned = [sb(f"turned{k}", [P, 2, GQ]) for k in range(3)]
        yT = [sb(f"yT{k}", [P, GQ]) for k in range(2)]
        ident = sb("ident", [P, P])
        ident_b = sb("ident_b", [P, P], BF16)
        mask = sb("mask", [P, P])
        mask_b = sb("mask_b", [P, P], BF16)
        w_d = sb("w_d", [C, C])
        w_qp = sb("w_qp", [C, P])
        w_kp = sb("w_kp", [C, P])
        w_vp = sb("w_vp", [C, P])
        w_op = sb("w_op", [P, C])
        negmax = sb("negmax", [P, NT, 2, 2])
        rowsum = sb("rowsum", [P, NT, 2, 2])
        lowest = sb("lowest", [P, NT, 2])
        shift = sb("shift", [P, NT, 2, 2])
        factor = sb("factor", [P, NT, 2, 2])
        part = sb("part", [P, NT, 2, 2])
        total = sb("total", [P, NT, 2])
        inverse = sb("inverse", [P, NT, 2])
        scales = sb("scales", [P, NT, 2, 2])
        wgu_n = sb("wgu_n", [P, 6, C])
        wd_n = sb("wd_n", [C, FF])
        wgu_T = sb("wgu_T", [C, 2, FF])
        wd_T = sb("wd_T", [P, 3, C])
        zn = [sb(f"zn{k}", [P, GT, C]) for k in range(3)]
        zq = sb("zq", [P, GT, C])
        gate_s = [sb(f"gate_s{k}", [P, GT, FF]) for k in range(2)]
        hid = [sb(f"hid{k}", [P, GT, FF]) for k in range(2)]
        WIDE = (GT * C, 6 * C)
        mag = [sb(f"mag{w}", [P, WIDE[w]]) for w in range(2)]
        qb = [sb(f"qb{w}", [P, WIDE[w]]) for w in range(2)]
        qc = [sb(f"qc{w}", [P, WIDE[w]]) for w in range(2)]
        amax = [sb(f"amax{w}", [P, WIDE[w] // BLK]) for w in range(2)]
        qscale = [sb(f"qscale{w}", [P, WIDE[w] // BLK]) for w in range(2)]
        stats = [sb(f"stats{w}", [P, NG, GT, 6]) for w in range(2)]
        mv = [sb(f"mv{w}", [P, NG, GT, 2]) for w in range(2)]
        veps = [sb(f"veps{w}", [P, NG, GT]) for w in range(2)]
        rstd = [sb(f"rstd{w}", [P, NG, GT]) for w in range(2)]
        neg_half = sb("neg_half", [P, GT])
        z2 = [sb(f"z2{k}", [P, GT, C]) for k in range(2)]
        res = [sb(f"res{k}", [P, GT, C]) for k in range(2)]

        slots = [psum(f"slot{b}", [P, 2, BANK]) for b in range(2)]
        tp = [psum(f"tp{b}", [P, 2, GQ]) for b in range(3)]
        yo_ps = psum("yo_ps", [P, 2, GQ])
        y_ps, o_ps = yo_ps[:, 0, :], yo_ps[:, 1, :]

        x_loaded = sem("x_loaded")
        wd_loaded = sem("wd_loaded")
        wqk_loaded = sem("wqk_loaded")
        wv_loaded = sem("wv_loaded")
        wo_loaded = sem("wo_loaded")
        ffw_loaded = sem("ffw_loaded")
        consts_made = sem("consts_made")
        consts_cast = sem("consts_cast")
        rows_cleared = sem("rows_cleared")
        slot_filled = sem("slot_filled")
        slot_free = [sem(f"slot_free{b}") for b in range(2)]
        max_ready = sem("max_ready")
        high_ready = sem("high_ready")
        stacks_loaded = [sem(f"stacks_loaded{s}") for s in range(2)]
        stat_step = sem("stat_step")
        lowest_ready = sem("lowest_ready")
        shift_ready = sem("shift_ready")
        factor_ready = sem("factor_ready")
        scales_ready = sem("scales_ready")
        rows_begun = sem("rows_begun")
        rows_scaled = sem("rows_scaled")
        turn_filled = sem("turn_filled")
        turn_copied = [sem(f"turn_copied{k}") for k in range(3)]
        y_filled = sem("y_filled")
        y_copied = sem("y_copied")
        o_filled = sem("o_filled")
        o_added = sem("o_added")
        norm_step = [sem(f"norm_step{w}") for w in range(2)]
        var_ready = [sem(f"var_ready{w}") for w in range(2)]
        rstd_ready = [sem(f"rstd_ready{w}") for w in range(2)]
        input_normed = sem("input_normed")
        mag_ready = [sem(f"mag_ready{w}") for w in range(2)]
        quant_step = [sem(f"quant_step{w}") for w in range(2)]
        on_grid = [sem(f"on_grid{w}") for w in range(2)]
        quantised = [sem(f"quantised{w}") for w in range(2)]
        silu_ready = sem("silu_ready")
        res_ready = sem("res_ready")
        stored = [sem(f"stored{k}") for k in range(2)]

        def slot_at(p, n):
            return p * SLOTS + (HEAD_SLOTS + n)

        def free_at(p, n):
            return p * (SLOTS // 2) + (HEAD_SLOTS // 2 + n // 2)

        def turns_copied(p, n):
            if n < 0:
                return p * (TURNS // 3) + ((n + TURNS) // 3 - TURNS // 3 + 2)
            return p * (TURNS // 3) + (n // 3 + 2)

        def ys_copied(p, n):
            return p * NG + (n + 1)

        def os_added(p, n):
            return p * NG + (n + 1)

        def flat(t):
            return t[:, :, :].rearrange("p a b -> p (a b)")

        block = ctx.enter_context(nc.Block())

        @block.sync
        def _(sp):
            for k in range(2):
                sp.dma_start(resid[:, k * 8:(k + 1) * 8, :], x_t[:, k * 8:(k + 1) * 8, :]).then_inc(x_loaded, 16)
            sp.dma_start(w_d[:, :], w_kv_down).then_inc(wd_loaded, 16)

            def load_qk(p):
                sp.dma_start(w_qp[:, :], w_q[:, bass.ds(p * P, P)]).then_inc(wqk_loaded, 16)
                sp.dma_start(w_kp[:, :], w_kv_up[:, bass.ds(p * P, P)]).then_inc(wqk_loaded, 16)

            def load_v(p):
                sp.dma_start(w_vp[:, :], w_kv_up[:, bass.ds(p * P + HD, P)]).then_inc(wv_loaded, 16)

            def load_o(p):
                sp.dma_start(w_op[:, :], w_out[bass.ds(p * P, P), :]).then_inc(wo_loaded, 16)

            def move_halves(w, s, b, uses):
                sp.wait_ge(slot_free[b], uses)
                cols = slice(s * CH, (s + 1) * CH)
                up, down = slice(0, HEAD), slice(HEAD, P)
                if w == "q":
                    moves = [(q_st[0], down, q_lo, up), (q_st[1], up, q_lo, down)]
                else:
                    moves = [(k_st[0], down, k_sw[0], up), (k_sw[0], down, k_st[0], up),
                             (k_st[1], up, k_sw[1], down), (k_sw[1], up, k_st[1], down)]
                for to, a, frm, b in moves:
                    sp.dma_start(to[a, cols].bitcast(F32), frm[b, cols].bitcast(F32)).then_inc(stacks_loaded[s], 16)

            load_qk(0)
            load_v(0)
            load_o(0)
            for n, (w, s) in enumerate(PROJECTIONS):
                move_halves(w, s, n % 2, 3 + n // 2)

            def body(p):
                sp.wait_ge(slot_filled, slot_at(p, 0))
                load_qk(p + 1)
                sp.wait_ge(slot_filled, slot_at(p, 2))
                load_v(p + 1)
                for it in pair:
                    if it[0] == "P":
                        move_halves(it[1], it[2], SLOT[it] % 2, free_at(p, SLOT[it]) + 1)
                sp.wait_ge(o_filled, p * NG + NG)
                load_o(p + 1)

            with sp.Fori(0, LAST) as p:
                body(p)
            for g in range(NG):
                sp.wait_ge(res_ready, g + 1)
                sp.dma_start(out_t[:, g * GT:(g + 1) * GT, :], res[g % 2][:, :, :]).then_inc(stored[g % 2], 16)
            for k in range(2):
                sp.wait_ge(stored[k], 16 * (NG // 2))

        @block.gpsimd
        def _(pool):
            pool.memset(ident[:, :], 0.0).then_inc(consts_made, 1)
            pool.memset(mask[:, :], 0.0).then_inc(consts_made, 1)
            pool.memset(neg_half[:, :], -0.5).then_inc(consts_made, 1)
            pool.wait_ge(consts_made, 3)
            pool.affine_select(out=ident[:, :], in_=ident[:, :], compare_op=ALU.not_equal, fill=1.0, base=0,
                               pattern=[[-1, P]], channel_multiplier=1).then_inc(consts_made, 1)
            pool.affine_select(out=mask[:, :], in_=mask[:, :], compare_op=ALU.is_ge, fill=MASKED, base=0,
                               pattern=[[-1, P]], channel_multiplier=1).then_inc(consts_made, 1)

            def scale_rows(p, i):
                pool.wait_ge(scales_ready, p * NT + i + 1)
                pool.sem_inc(rows_begun, 1)
                buf = probs[(i // GT) % 2]
                for c, (a, n) in enumerate(chunks(i)):
                    for h in range(2):
                        row = buf[:, i % GT, h, a:a + n]
                        pool.tensor_scalar(row, row, scales[:, i, h, c:c + 1], 1.0, ALU.mult,
                                           ALU.mult).then_inc(rows_scaled, 1)

            def rsqrt(w, g):
                pool.wait_ge(var_ready[w], g + 1)
                pool.tensor_tensor(rstd[w][:, g, :], veps[w][:, g, :], neg_half[:, :],
                                   ALU.pow).then_inc(rstd_ready[w], 1)

            def finish(w, q, dst, n):
                def blocks(t):
                    return t[:, 0:n].rearrange("p (b k) -> p b k", k=BLK)
                pool.wait_ge(on_grid[w], q + 1)
                pool.tensor_tensor(blocks(dst), blocks(mag[w]),
                                   qscale[w][:, 0:n // BLK].unsqueeze(2).to_broadcast([P, n // BLK, BLK]),
                                   ALU.mult).then_inc(quantised[w], 1)

            def body(p, plan):
                for it in plan:
                    if it[0] == "N":
                        scale_rows(p, it[1])
                    elif it[0] == "norm" and it[3] == 2:
                        rsqrt(it[1], it[2])
                    elif it[0] == "quant" and it[3] == QSTEPS - 1:
                        w, g = it[1:3]
                        finish(w, (0, 2)[w] + g, flat((zq, hid[g % 2])[w]), (GT * C, GT * FF)[w])

            finish(1, 0, flat(wgu_n), 6 * C)
            finish(1, 1, wd_n[:, :], FF)
            with pool.Fori(0, LAST) as p:
                body(p, pair)
            body(LAST, final)

        @block.scalar
        def _(act):
            def xT_copy(s):
                act.wait_ge(slot_filled, s + 1)
                act.copy(xT[:, s * CH:(s + 1) * CH], slots[s % 2][:, :, :]).then_inc(slot_free[s % 2], 1)

            def latent_copy(s):
                act.wait_ge(slot_filled, 2 + s + 1)
                act.copy(latT[:, s * CH:(s + 1) * CH], slots[s % 2][:, :, :]).then_inc(slot_free[s % 2], 1)

            def high_parts(p, w, s, filled, b):
                act.wait_ge(slot_filled, filled + 1)
                stack = q_st if w == "q" else k_st
                scale = SCALE if w == "q" else 1.0
                cols = slice(s * CH, (s + 1) * CH)
                for h in range(2):
                    rows = slice(h * HEAD, (h + 1) * HEAD)
                    act.activation(stack[h][rows, cols], slots[b][rows, :, :], ACT.Copy,
                                   scale=scale).then_inc(high_ready, 1)

            def values(p, s):
                act.wait_ge(slot_filled, slot_at(p, s) + 1)
                act.copy(v[:, s * 8:(s + 1) * 8, :], slots[s % 2][:, :, :]).then_inc(slot_free[s % 2], 1)

            def exp_chunk(p, it, n, k):
                _, i, parts = it
                act.wait_ge(max_ready, p * CHUNKS + k + 1)
                for b, (h, c) in enumerate(parts):
                    a, width = chunks(i)[c]
                    scores = slots[n % 2][:, b:, :].rearrange("p a b -> p (a b)")[:, 0:width]
                    ins = act.activation(probs[(i // GT) % 2][:, i % GT, h, a:a + width], scores, ACT.Exp,
                                         bias=negmax[:, i, h, c:c + 1], scale=1.0,
                                         accum_out=rowsum[:, i, h, c:c + 1])
                ins.then_inc(slot_free[n % 2], 1)

            def factors(p, i):
                act.wait_ge(shift_ready, p * len(TWO) + TWO.index(i) + 1)
                act.activation(factor[:, i, :, :], shift[:, i, :, :], ACT.Exp).then_inc(factor_ready, 1)

            def turn_copy(p, g, j, n):
                act.wait_ge(turn_filled, p * TURNS + n + 1)
                lo = 0 if j <= GT * g else P
                act.copy(turned[n % 3][:, :, lo:GQ], tp[n % 3][:, :, lo:GQ]).then_inc(turn_copied[n % 3], 1)

            def y_copy(p, g):
                act.wait_ge(y_filled, p * NG + g + 1)
                act.copy(yT[g % 2][:, :], y_ps).then_inc(y_copied, 1)

            def body(p, plan, slot, turn, chunk):
                for it in plan:
                    if it[0] == "V":
                        values(p, it[1])
                    elif it[0] == "S":
                        exp_chunk(p, it, slot[it], chunk[it])
                    elif it[0] == "F":
                        factors(p, it[1])
                    elif it[0] == "T" and turn[it[1:]] % 3 != 2:
                        turn_copy(p, it[1], it[2], turn[it[1:]])
                    elif it[0] == "M" and it[2] == GT * it[1] + GT - 1:
                        y_copy(p, it[1])
                    elif it[0] == "P":
                        high_parts(p + 1, it[1], it[2], slot_at(p, slot[it]), slot[it] % 2)
                    elif it[0] == "abs":
                        w, g = it[1:]
                        if w == 0:
                            act.wait_ge(input_normed, g + 1)
                            magnitudes(0, g, flat(zn[g % 3]), GT * C)
                        else:
                            for t in range(GT):
                                m = slot[("up", g, t)]
                                act.wait_ge(slot_free[m % 2], free_at(p, m) + 1)
                            magnitudes(1, 2 + g, flat(hid[g % 2]), GT * FF)
                    elif it[0] == "turn":
                        feed_turned(p, it, turn)
                    elif it[0] == "up":
                        feed_gate(p, it[1], slot)

            def magnitudes(w, q, src, n):
                if q > 0:
                    act.wait_ge(quantised[w], q)
                act.activation(mag[w][:, 0:n], src, ACT.Abs).then_inc(mag_ready[w], 1)

            def feed_turned(p, it, turn):
                for t in range(1 + it[1]):
                    n = turn[it + (t,)]
                    act.wait_ge(turn_filled, p * TURNS + n + 1)
                    if it[1] == 0:
                        act.copy(turned[n % 3][:, 0, :], tp[n % 3][:, 0, :]).then_inc(turn_copied[n % 3], 1)
                    else:
                        to, bank = flat(turned[n % 3]), flat(tp[n % 3])
                        act.copy(to[:, 0:256], bank[:, 0:256])
                        act.copy(to[0:96, 256:384], bank[0:96, 256:384]).then_inc(turn_copied[n % 3], 1)

            def feed_gate(p, g, slot):
                for t in range(GT):
                    m = slot[("up", g, t)]
                    act.wait_ge(slot_filled, slot_at(p, m) + 1)
                    act.activation(gate_s[g % 2][:, t, :], slots[m % 2][:, 0, 0:FF],
                                   ACT.Silu).then_inc(silu_ready, 1)

            act.dma_start(wgu_n[:, 0:2, :], w_gate[0:256, :].rearrange("(n p) c -> p n c", p=P)).then_inc(ffw_loaded, 16)
            act.dma_start(wgu_n[0:96, 2, :], w_gate[256:FF, :]).then_inc(ffw_loaded, 16)
            act.dma_start(wgu_n[:, 3:5, :], w_up[0:256, :].rearrange("(n p) c -> p n c", p=P)).then_inc(ffw_loaded, 16)
            act.dma_start(wgu_n[0:96, 5, :], w_up[256:FF, :]).then_inc(ffw_loaded, 16)
            act.dma_start(wd_n[:, :], w_down).then_inc(ffw_loaded, 16)
            act.wait_ge(ffw_loaded, 16 * 5)
            act.wait_ge(rows_cleared, 2)
            magnitudes(1, 0, flat(wgu_n), 6 * C)
            act.sem_inc(turn_copied[0], 1)
            act.sem_inc(turn_copied[1], 1)
            act.sem_inc(y_copied, 1)
            xT_copy(0)
            xT_copy(1)
            latent_copy(0)
            latent_copy(1)
            for n, (w, s) in enumerate(PROJECTIONS):
                high_parts(0, w, s, 4 + n, n % 2)
                if n == 1:
                    magnitudes(1, 1, wd_n[:, :], FF)
            act.wait_ge(slot_filled, 9)
            act.copy(wgu_T[:, :, :], slots[0][:, :, 0:FF]).then_inc(slot_free[0], 1)
            act.wait_ge(slot_filled, 10)
            act.copy(flat(wd_T)[:, 0:256], slots[1][:, 0, 0:256])
            act.copy(wd_T[0:96, 2, :], slots[1][0:96, 0, 256:384]).then_inc(slot_free[1], 1)
            with act.Fori(0, LAST) as p:
                body(p, later(pair, "S", ACT_LATE), SLOT, TURN, CHUNK)
            body(LAST, later(final, "S", ACT_LATE), FSLOT, FTURN, FCHUNK)

        @block.vector
        def _(dve):
            dve.memset(wgu_n[96:P, 2, :], 0.0).then_inc(rows_cleared, 1)
            dve.memset(wgu_n[96:P, 5, :], 0.0).then_inc(rows_cleared, 1)
            dve.wait_ge(consts_made, 5)
            dve.tensor_copy(ident_b[:, :], ident[:, :]).then_inc(consts_cast, 1)
            dve.tensor_copy(mask_b[:, :], mask[:, :]).then_inc(consts_cast, 1)
            dve.sem_inc(turn_copied[2], 1)
            dve.sem_inc(o_added, 1)
            def low_parts(p, w, s, b):
                n = PROJECTIONS.index((w, s))
                cols = slice(s * CH, (s + 1) * CH)
                scale = SCALE if w == "q" else 1.0
                stack = q_st if w == "q" else k_st
                dve.wait_ge(high_ready, p * 8 + 2 * n + 2)
                ps = slots[b][:, :, :].rearrange("p a b -> p (a b)")
                for h in range(2):
                    rows = slice(h * HEAD, (h + 1) * HEAD)
                    to = q_lo if w == "q" else k_sw[h]
                    ins = dve.scalar_tensor_tensor(out=to[rows, cols], in0=ps[rows, :], scalar=scale,
                                                   in1=stack[h][rows, cols].bitcast(F32),
                                                   op0=ALU.mult, op1=ALU.subtract)
                ins.then_inc(slot_free[b], 1)

            def chunk_max(p, it, n):
                _, i, parts = it
                h, c = parts[0]
                width = chunks(i)[c][1]
                dve.wait_ge(slot_filled, slot_at(p, n) + 1)
                if len(parts) == 2:
                    to, frm = negmax[:, i, :, c], slots[n % 2][:, :, 0:width]
                else:
                    to = negmax[:, i, h, c:c + 1]
                    frm = slots[n % 2][:, :, :].rearrange("p a b -> p (a b)")[:, 0:width]
                dve.tensor_reduce(to, frm, AX.X, ALU.max, negate=True).then_inc(max_ready, 1)

            def shifts(p, i, k):
                dve.wait_ge(max_ready, p * CHUNKS + k + 1)
                dve.tensor_reduce(lowest[:, i, :], negmax[:, i, :, :], AX.X, ALU.min).then_inc(lowest_ready, 1)
                dve.wait_ge(lowest_ready, p * len(TWO) + TWO.index(i) + 1)
                dve.tensor_tensor(shift[:, i, :, :], lowest[:, i, :].unsqueeze(2).to_broadcast([P, 2, 2]),
                                  negmax[:, i, :, :], ALU.subtract).then_inc(shift_ready, 1)

            def row_scales(p, i, n):
                if i not in TWO:
                    dve.wait_ge(slot_free[n % 2], free_at(p, n) + 1)
                    dve.reciprocal(scales[:, i, :, 0], rowsum[:, i, :, 0]).then_inc(scales_ready, 1)
                    return
                base = p * (3 * len(TWO)) + 3 * TWO.index(i)
                dve.wait_ge(factor_ready, p * len(TWO) + TWO.index(i) + 1)
                dve.tensor_tensor(part[:, i, :, :], factor[:, i, :, :], rowsum[:, i, :, :],
                                  ALU.mult).then_inc(stat_step, 1)
                dve.wait_ge(stat_step, base + 1)
                dve.tensor_reduce(total[:, i, :], part[:, i, :, :], AX.X, ALU.add).then_inc(stat_step, 1)
                dve.wait_ge(stat_step, base + 2)
                dve.reciprocal(inverse[:, i, :], total[:, i, :]).then_inc(stat_step, 1)
                dve.wait_ge(stat_step, base + 3)
                dve.tensor_tensor(scales[:, i, :, :], factor[:, i, :, :],
                                  inverse[:, i, :].unsqueeze(2).to_broadcast([P, 2, 2]),
                                  ALU.mult).then_inc(scales_ready, 1)

            def turn_copy(p, g, j, n):
                dve.wait_ge(turn_filled, p * TURNS + n + 1)
                lo = 0 if j <= GT * g else P
                dve.tensor_copy(turned[n % 3][:, :, lo:GQ], tp[n % 3][:, :, lo:GQ]).then_inc(turn_copied[n % 3], 1)

            def add_output(p, g):
                dve.wait_ge(o_filled, p * NG + g + 1)
                dst = resid[:, g * GT:(g + 1) * GT, :].rearrange("p a b -> p (a b)")
                dve.tensor_tensor(dst, o_ps, dst, ALU.add).then_inc(o_added, 1)

            def quantise(w, q, src, n, s):
                nb = n // BLK
                def blocks(t):
                    return t[:, 0:n].rearrange("p (b k) -> p b k", k=BLK)
                a, b, c = (t[w][:, 0:n] for t in (mag, qb, qc))
                top, scale = amax[w][:, 0:nb], qscale[w][:, 0:nb]
                if s == 0:
                    dve.wait_ge(mag_ready[w], q + 1)
                    dve.tensor_reduce(top, blocks(mag[w]), AX.X, ALU.max).then_inc(quant_step[w], 1)
                    return
                dve.wait_ge(quant_step[w], (QSTEPS - 1) * q + s)
                if s == 1:
                    ins = dve.tensor_scalar(scale, top, 1.0 / FP4_MAX, 1e-12, ALU.mult, ALU.max)
                elif s == 2:
                    ins = dve.reciprocal(top, scale)
                elif s == 3:
                    ins = dve.scalar_tensor_tensor(out=blocks(mag[w]), in0=blocks(mag[w]), scalar=BELOW_ONE,
                                                   in1=top.unsqueeze(2).to_broadcast([P, nb, BLK]),
                                                   op0=ALU.mult, op1=ALU.mult)
                elif s == 4:
                    ins = dve.tensor_scalar(b, a, 1.0, SPLITTER, ALU.max, ALU.mult)
                elif s == 5:
                    ins = dve.scalar_tensor_tensor(out=c, in0=a, scalar=1.0, in1=b, op0=ALU.max,
                                                   op1=ALU.subtract)
                elif s == 6:
                    ins = dve.tensor_tensor(b, b, c, ALU.add)
                elif s == 7:
                    ins = dve.tensor_scalar(c, a, 1.0, HALF_MAGIC, ALU.min, ALU.add)
                elif s == 8:
                    ins = dve.scalar_tensor_tensor(out=a, in0=c, scalar=HALF_MAGIC + 1.0, in1=b,
                                                   op0=ALU.subtract, op1=ALU.add)
                else:
                    dve.scalar_tensor_tensor(out=a.bitcast(U32), in0=src.bitcast(U32), scalar=0x80000000,
                                             in1=a.bitcast(U32), op0=ALU.bitwise_and,
                                             op1=ALU.bitwise_or).then_inc(on_grid[w], 1)
                    return
                ins.then_inc(quant_step[w], 1)

            def layer_norm(w, g, s):
                src = resid[:, g * GT:(g + 1) * GT, :] if w == 0 else z2[g % 2]
                dst = zn[g % 3] if w == 0 else res[g % 2]
                if s == 0:
                    if w == 0:
                        dve.wait_ge(o_added, os_added(LAST, g + 1))
                    else:
                        m = FSLOT[("down", g)]
                        dve.wait_ge(slot_free[m % 2], free_at(LAST, m) + 1)
                    for t in range(GT):
                        dve.bn_stats(stats[w][:, g, t, :], src[:, t, :]).then_inc(norm_step[w], 1)
                elif s == 1:
                    dve.wait_ge(norm_step[w], 4 * g + 2)
                    for t in range(GT):
                        dve.bn_aggr(mv[w][:, g, t, :], stats[w][:, g, t, :]).then_inc(norm_step[w], 1)
                elif s == 2:
                    dve.wait_ge(norm_step[w], 4 * g + 4)
                    dve.tensor_scalar(veps[w][:, g, :], mv[w][:, g, :, 1], EPS, None,
                                      ALU.add).then_inc(var_ready[w], 1)
                else:
                    dve.wait_ge(rstd_ready[w], g + 1)
                    if w == 1 and g >= 2:
                        dve.wait_ge(stored[g % 2], 16 * (g // 2))
                    for t in range(GT):
                        ins = dve.tensor_scalar(dst[:, t, :], src[:, t, :], mv[w][:, g, t, 0:1],
                                                rstd[w][:, g, t:t + 1], ALU.subtract, ALU.mult)
                    ins.then_inc((input_normed, res_ready)[w], 1)

            def product(p, g, slot):
                for t in range(GT):
                    m = slot[("up", g, t)]
                    dve.wait_ge(silu_ready, GT * g + t + 1)
                    ins = dve.tensor_tensor(hid[g % 2][:, t, :], slots[m % 2][:, 1, 0:FF], gate_s[g % 2][:, t, :],
                                            ALU.mult)
                    ins.then_inc(slot_free[m % 2], 1)

            def output_sum(p, g, slot):
                m = slot[("down", g)]
                dve.wait_ge(slot_filled, slot_at(p, m) + 1)
                dve.tensor_tensor(z2[g % 2][:, :, :], slots[m % 2][:, :, 0:C], zn[g % 3][:, :, :],
                                  ALU.add).then_inc(slot_free[m % 2], 1)

            def body(p, plan, slot, turn, chunk):
                for it in plan:
                    if it[0] == "S":
                        chunk_max(p, it, slot[it])
                    elif it[0] == "F":
                        shifts(p, it[1], chunk[("S", it[1], row_slots(it[1])[-1])])
                    elif it[0] == "N":
                        row_scales(p, it[1], slot[("S", it[1], row_slots(it[1])[-1])])
                    elif it[0] == "T" and turn[it[1:]] % 3 == 2:
                        turn_copy(p, it[1], it[2], turn[it[1:]])
                    elif it[0] == "O":
                        add_output(p, it[1])
                    elif it[0] == "P":
                        low_parts(p + 1, it[1], it[2], slot[it] % 2)
                    elif it[0] == "norm":
                        layer_norm(*it[1:])
                    elif it[0] == "quant":
                        w, g, s = it[1:]
                        quantise(w, (0, 2)[w] + g, flat((zn[g % 3], hid[g % 2])[w]), (GT * C, GT * FF)[w], s)
                    elif it[0] == "product":
                        product(p, it[1], slot)
                    elif it[0] == "sum":
                        output_sum(p, it[1], slot)

            for s in range(QSTEPS):
                quantise(1, 0, flat(wgu_n), 6 * C, s)
            for n, (w, s) in enumerate(PROJECTIONS):
                low_parts(0, w, s, n % 2)
            for s in range(QSTEPS):
                quantise(1, 1, wd_n[:, :], FF, s)
            with dve.Fori(0, LAST) as p:
                body(p, later(pair, "S", DVE_LATE), SLOT, TURN, CHUNK)
            body(LAST, later(final, "S", DVE_LATE), FSLOT, FTURN, FCHUNK)

        @block.tensor
        def _(pe):
            def slot_reusable(p, n):
                pe.wait_ge(slot_free[n % 2], free_at(p, n))

            def project(w, s, b, lhs, rhs):
                for k in range(2):
                    a = s * CH + k * BANK
                    ins = pe.matmul(slots[b][:, k, :], lhs[:, :], rhs[:, a:a + BANK], start=True, stop=True)
                ins.then_inc(slot_filled, 1)

            def values(p, s, n):
                slot_reusable(p, n)
                pe.wait_ge(wv_loaded, (p + 1) * 16)
                for t in range(8):
                    j = s * 8 + t
                    ins = pe.matmul(slots[n % 2][:, t // 4, (t % 4) * P:(t % 4 + 1) * P],
                                    latT[:, j * P:(j + 1) * P], w_vp[:, :], start=True, stop=True)
                ins.then_inc(slot_filled, 1)

            def scores(p, it, n):
                _, i, parts = it
                slot_reusable(p, n)
                for bank, (h, c) in enumerate(parts):
                    a, width = chunks(i)[c]
                    q = q_st[h][:, i * P:(i + 1) * P]
                    for b in range(0, width, BANK):
                        m = min(BANK, width - b)
                        end = a + b + m == (i + 1) * P
                        at = bank + b // BANK
                        keys = slice(a + b, a + b + m)
                        pe.matmul(slots[n % 2][:, at, 0:m], q, k_st[h][:, keys], start=True, stop=False)
                        ins = pe.matmul(slots[n % 2][:, at, 0:m], q, k_sw[h][:, keys], start=False, stop=not end)
                        if end:
                            ins = pe.matmul(slots[n % 2][:, at, m - P:m], ident_b[:, :], mask_b[:, :],
                                            start=False, stop=True)
                ins.then_inc(slot_filled, 1)

            def turn(p, g, j, n, scaled):
                pe.wait_ge(turn_copied[n % 3], turns_copied(p, n - 3))
                i = GT * g + GT - 1
                pe.wait_ge(rows_scaled, p * NORMS + scaled[(i, 1, j * P // CH)])
                lo = 0 if j <= GT * g else 1
                for h in range(2):
                    for t in range(lo, GT):
                        ins = pe.transpose(tp[n % 3][:, h, t * P:(t + 1) * P],
                                           probs[g % 2][:, t, h, j * P:(j + 1) * P], ident[:, :])
                ins.then_inc(turn_filled, 1)

            def times_values(p, g, j, n):
                pe.wait_ge(turn_copied[n % 3], turns_copied(p, n))
                last = GT * g + GT - 1
                lo = 0 if j <= GT * g else P
                for h in range(2):
                    ins = pe.matmul(y_ps[h * HEAD:(h + 1) * HEAD, lo:GQ], v[:, j, h * HEAD:(h + 1) * HEAD],
                                    turned[n % 3][:, h, lo:GQ], start=(j == 0), stop=(j == last))
                if j == last:
                    ins.then_inc(y_filled, 1)

            def project_out(p, g):
                pe.wait_ge(y_copied, ys_copied(p, g + 1))
                pe.wait_ge(wo_loaded, (p + 1) * 16)
                for t in range(GT):
                    ins = pe.matmul(o_ps[:, t * P:(t + 1) * P], yT[g % 2][:, t * P:(t + 1) * P], w_op[:, :],
                                    start=True, stop=True)
                ins.then_inc(o_filled, 1)

            def bank_free(p, n):
                pe.wait_ge(turn_copied[n % 3], turns_copied(p, n - 3))

            def turn_weights():
                pe.wait_ge(quantised[1], 1)
                pe.wait_ge(slot_free[0], 4)
                for w in range(2):
                    for k, (a, m) in enumerate(FFK):
                        ins = pe.transpose(slots[0][:, w, a:a + m], wgu_n[0:m, 3 * w + k, :], ident[0:m, 0:m])
                ins.then_inc(slot_filled, 1)
                pe.wait_ge(quantised[1], 2)
                pe.wait_ge(slot_free[1], 4)
                for k, (a, m) in enumerate(FFK):
                    ins = pe.transpose(slots[1][0:m, 0, k * P:(k + 1) * P], wd_n[:, a:a + m], ident[:, :])
                ins.then_inc(slot_filled, 1)

            def feed_turn(p, w, g, turns):
                pe.wait_ge(quantised[w], (0, 2)[w] + g + 1)
                for t in range(1 + w):
                    n = turns[("turn", w, g, t)]
                    bank_free(p, n)
                    if w == 0:
                        for k in range(GT):
                            ins = pe.transpose(tp[n % 3][:, 0, k * P:(k + 1) * P], zq[:, k, :], ident[:, :])
                    else:
                        for k, (a, m) in enumerate(FFK):
                            ins = pe.transpose(flat(tp[n % 3])[0:m, k * P:(k + 1) * P], hid[g % 2][:, t, a:a + m],
                                               ident[:, :])
                    ins.then_inc(turn_filled, 1)

            def feed_up(p, g, slot, turns):
                n = turns[("turn", 0, g, 0)]
                pe.wait_ge(turn_copied[n % 3], turns_copied(p, n))
                for t in range(GT):
                    m = slot[("up", g, t)]
                    slot_reusable(p, m)
                    for k in range(2):
                        ins = pe.matmul(slots[m % 2][:, k, 0:FF], turned[n % 3][:, 0, t * P:(t + 1) * P],
                                        wgu_T[:, k, :], start=True, stop=True)
                    ins.then_inc(slot_filled, 1)

            def feed_down(p, g, slot, turns):
                m = slot[("down", g)]
                slot_reusable(p, m)
                for t in range(GT):
                    n = turns[("turn", 1, g, t)]
                    pe.wait_ge(turn_copied[n % 3], turns_copied(p, n))
                    for k, (a, w) in enumerate(FFK):
                        ins = pe.matmul(slots[m % 2][:, t, 0:C], flat(turned[n % 3])[0:w, k * P:(k + 1) * P],
                                        wd_T[0:w, k, :], start=(k == 0), stop=(k == 2))
                ins.then_inc(slot_filled, 1)

            def body(p, plan, slot, turns, scaled):
                for it in plan:
                    if it[0] == "V":
                        values(p, it[1], slot[it])
                    elif it[0] == "S":
                        if it[1] in (0, NT // 2) and it[2][0] == (0, 0):
                            pe.wait_ge(stacks_loaded[it[1] // (NT // 2)], (p + 1) * (16 * 6))
                        scores(p, it, slot[it])
                    elif it[0] == "T":
                        g, j = it[1:]
                        turn(p, g, j, turns[(g, j)], scaled)
                    elif it[0] == "M":
                        g, j = it[1:]
                        if j == 0:
                            pe.wait_ge(o_added, os_added(p, g))
                            if g == 0:
                                pe.wait_ge(slot_free[1], free_at(p, 1) + 1)
                        times_values(p, g, j, turns[(g, j)])
                    elif it[0] == "O":
                        project_out(p, it[1])
                    elif it[0] == "P":
                        slot_reusable(p, slot[it])
                        if it[1:] == ("q", 0):
                            pe.wait_ge(wqk_loaded, (p + 2) * 32)
                        w, rhs = (w_qp, xT) if it[1] == "q" else (w_kp, latT)
                        project(it[1], it[2], slot[it] % 2, w, rhs)
                    elif it[0] == "turn":
                        feed_turn(p, it[1], it[2], turns)
                    elif it[0] == "up":
                        feed_up(p, it[1], slot, turns)
                    elif it[0] == "down":
                        feed_down(p, it[1], slot, turns)

            pe.wait_ge(consts_made, 5)
            for s in range(2):
                pe.wait_ge(x_loaded, 32)
                for t in range(8):
                    ins = pe.transpose(slots[s][:, t // 4, (t % 4) * P:(t % 4 + 1) * P], resid[:, s * 8 + t, :],
                                       ident[:, :])
                ins.then_inc(slot_filled, 1)
            pe.wait_ge(wd_loaded, 16)
            for s in range(2):
                pe.wait_ge(slot_free[s], 1)
                project("l", s, s, w_d, xT)
            pe.wait_ge(wqk_loaded, 32)
            for n, (w, s) in enumerate(PROJECTIONS):
                pe.wait_ge(slot_free[n % 2], 2 + n // 2)
                project(w, s, n % 2, *((w_qp, xT) if w == "q" else (w_kp, latT)))
            turn_weights()
            pe.wait_ge(consts_cast, 2)
            with pe.Fori(0, LAST) as p:
                body(p, pair, SLOT, TURN, SCALED)
            body(LAST, final, FSLOT, FTURN, FSCALED)


_INS = ["L0_attn_x", "L0_attn_w_kv_down", "L0_attn_w_kv_up", "L0_attn_w_q", "L0_attn_w_out",
        "L0_ffn_w_gate", "L0_ffn_w_up", "L0_ffn_w_down"]
_OUTS = [((1, 2048, 128), "float32")]


def kernel(**inputs):
    import numpy as _np
    import concourse.bacc as _bacc
    from concourse import mybir as _mybir
    from concourse.bass_utils import run_bass_kernel_spmd as _run

    nc = _bacc.Bacc("TRN2", target_bir_lowering=False, num_devices=1)
    arrays, args = {}, []
    for name in _INS:
        a = _np.ascontiguousarray(inputs[name])
        arrays[f"in_{name}_dram"] = a
        args.append(nc.dram_tensor(f"in_{name}_dram", a.shape, _mybir.dt.from_np(a.dtype), kind="ExternalInput").ap())
    for i, (shape, dtype) in enumerate(_OUTS):
        dt = _mybir.dt.from_np(_np.dtype(dtype))
        args.append(nc.dram_tensor(f"out_{i}_dram", shape, dt, kind="ExternalOutput").ap())
    block_kernel(nc, *args)
    r = _run(nc, [arrays], core_ids=[0])
    got = tuple(r.results[0][f"out_{i}_dram"] for i in range(len(_OUTS)))
    return got[0]
```
